# Optimizing a Trainium2 kernel written in Bass

```python
import numpy as np
import jax
import jax.numpy as jnp

def _softmax(x, axis=-1):
    return jax.nn.softmax(x, axis=axis)

def _gelu(x):
    return jax.nn.gelu(x, approximate=True)

def _silu(x):
    return jax.nn.silu(x)

def _sigmoid(x):
    return jax.nn.sigmoid(x)

def _layernorm(x, axis=-1, eps=1e-05):
    m = jnp.mean(x, axis=axis, keepdims=True)
    v = jnp.var(x, axis=axis, keepdims=True)
    return (x - m) / jnp.sqrt(v + eps)

def _scatter_add(tgt, idx, src, axis=0):
    return tgt.at[idx].add(src)

def _segment_sum(src, seg, n):
    return jax.ops.segment_sum(src, seg, n)
kernel_name = 'mk_sandwich_d2_jaxref_r8_121982'

def setup_inputs(seed: int=0):
    np.random.seed(seed)
    _w = jnp.asarray

    def _L0_attn_setup():
        import jax, jax.numpy as jnp
        import numpy as np
        D_MODEL, D_QKV, N_HEADS = (128, 64, 16)
        key = jax.random.key(seed)
        k_x, k_qkv, k_out = jax.random.split(key, 3)
        X = jax.random.normal(k_x, (2, 256, D_MODEL), dtype=jnp.float32)
        W_qkv = jax.random.normal(k_qkv, (D_MODEL, 3 * D_QKV * N_HEADS), dtype=jnp.float32) * D_MODEL ** (-0.5)
        W_out = jax.random.normal(k_out, (D_QKV * N_HEADS, D_MODEL), dtype=jnp.float32) * (D_QKV * N_HEADS) ** (-0.5)
        return {'X': X, 'W_qkv': W_qkv, 'W_out': W_out}
    _L0_attn_in = _L0_attn_setup()

    def _L0_ffn_setup():
        import jax, jax.numpy as jnp
        import numpy as np
        D, H, O, E, TOPK = (128, 512, 128, 8, 2)
        B, S = (4, 128)
        key = jax.random.key(seed)
        ks = jax.random.split(key, 12)
        std = 0.02
        return {'hidden_states': jax.random.normal(ks[0], (B, S, D), dtype=jnp.float32), 'norm_weight': jnp.ones((D,), dtype=jnp.float32), 'router_w': jax.random.normal(ks[1], (E, D), dtype=jnp.float32) * std, 'sw1': jax.random.normal(ks[2], (D, H), dtype=jnp.float32) * (1.0 / np.sqrt(D)), 'sb1': jnp.zeros((H,), dtype=jnp.float32), 'sw2': jax.random.normal(ks[3], (H, O), dtype=jnp.float32) * (1.0 / np.sqrt(H)), 'sb2': jnp.zeros((O,), dtype=jnp.float32), 'ew1': jax.random.normal(ks[4], (E, D, H), dtype=jnp.float32) * (1.0 / np.sqrt(D)), 'eb1': jnp.zeros((E, H), dtype=jnp.float32), 'ew2': jax.random.normal(ks[5], (E, H, O), dtype=jnp.float32) * (1.0 / np.sqrt(H)), 'eb2': jnp.zeros((E, O), dtype=jnp.float32)}
    _L0_ffn_in = _L0_ffn_setup()

    def _L1_attn_setup():
        import jax, jax.numpy as jnp
        import numpy as np
        import math
        NUM_HEADS = 8
        D_HEAD = 128
        DEPTH = 1
        LAMBDA_INIT = 0.8 - 0.6 * math.exp(-0.3 * DEPTH)
        EPS = 1e-05
        key = jax.random.key(seed)
        ks = jax.random.split(key, 10)
        B, N, D = (2, 256, 128)
        s = 0.02
        return {'X': jax.random.normal(ks[0], (B, N, D), jnp.float32), 'Wq': jax.random.normal(ks[1], (2 * D_HEAD * NUM_HEADS, D), jnp.float32) * s, 'Wk': jax.random.normal(ks[2], (2 * D_HEAD * NUM_HEADS, D), jnp.float32) * s, 'Wv': jax.random.normal(ks[3], (2 * D_HEAD * NUM_HEADS, D), jnp.float32) * s, 'Wo': jax.random.normal(ks[4], (D, 2 * D_HEAD * NUM_HEADS), jnp.float32) * s, 'lambda_q1': jax.random.normal(ks[5], (NUM_HEADS, D_HEAD), jnp.float32) * 0.1, 'lambda_k1': jax.random.normal(ks[6], (NUM_HEADS, D_HEAD), jnp.float32) * 0.1, 'lambda_q2': jax.random.normal(ks[7], (NUM_HEADS, D_HEAD), jnp.float32) * 0.1, 'lambda_k2': jax.random.normal(ks[8], (NUM_HEADS, D_HEAD), jnp.float32) * 0.1, 'rms_scale': jnp.ones((2 * D_HEAD,), jnp.float32)}
    _L1_attn_in = _L1_attn_setup()

    def _L1_ffn_setup():
        import jax, jax.numpy as jnp
        import numpy as np
        D_IN, D_HID = (128, 512)

        def _ternary(key, shape):
            return jax.random.randint(key, shape, -1, 2).astype(jnp.float32)

        def _tlin(x, w, s):
            return jnp.einsum('bsi,oi->bso', x, w) * s
        key = jax.random.key(seed)
        ks = jax.random.split(key, 12)
        inv = lambda fan: 1.0 / np.sqrt(fan).astype(np.float32)
        return {'x': jax.random.normal(ks[0], (4, 256, D_IN), dtype=jnp.float32), 'w1_w': _ternary(ks[1], (D_HID, D_IN)), 'w1_s': jax.random.uniform(ks[2], (D_HID,), dtype=jnp.float32) * inv(D_IN), 'w2_w': _ternary(ks[3], (D_HID, D_IN)), 'w2_s': jax.random.uniform(ks[4], (D_HID,), dtype=jnp.float32) * inv(D_IN), 'h1_w': _ternary(ks[5], (D_HID, D_HID)), 'h1_s': jax.random.uniform(ks[6], (D_HID,), dtype=jnp.float32) * inv(D_HID), 'h2_w': _ternary(ks[7], (D_HID, D_HID)), 'h2_s': jax.random.uniform(ks[8], (D_HID,), dtype=jnp.float32) * inv(D_HID), 'w3_w': _ternary(ks[9], (D_IN, D_HID)), 'w3_s': jax.random.uniform(ks[10], (D_IN,), dtype=jnp.float32) * inv(D_HID)}
    _L1_ffn_in = _L1_ffn_setup()
    _d = {'L0_attn_X': _L0_attn_in['X'], 'L0_attn_W_qkv': _L0_attn_in['W_qkv'], 'L0_attn_W_out': _L0_attn_in['W_out'], 'L0_ffn_norm_weight': _L0_ffn_in['norm_weight'], 'L0_ffn_router_w': _L0_ffn_in['router_w'], 'L0_ffn_sw1': _L0_ffn_in['sw1'], 'L0_ffn_sb1': _L0_ffn_in['sb1'], 'L0_ffn_sw2': _L0_ffn_in['sw2'], 'L0_ffn_sb2': _L0_ffn_in['sb2'], 'L0_ffn_ew1': _L0_ffn_in['ew1'], 'L0_ffn_eb1': _L0_ffn_in['eb1'], 'L0_ffn_ew2': _L0_ffn_in['ew2'], 'L0_ffn_eb2': _L0_ffn_in['eb2'], 'L1_attn_Wq': _L1_attn_in['Wq'], 'L1_attn_Wk': _L1_attn_in['Wk'], 'L1_attn_Wv': _L1_attn_in['Wv'], 'L1_attn_Wo': _L1_attn_in['Wo'], 'L1_attn_lambda_q1': _L1_attn_in['lambda_q1'], 'L1_attn_lambda_k1': _L1_attn_in['lambda_k1'], 'L1_attn_lambda_q2': _L1_attn_in['lambda_q2'], 'L1_attn_lambda_k2': _L1_attn_in['lambda_k2'], 'L1_attn_rms_scale': _L1_attn_in['rms_scale'], 'L1_ffn_w1_w': _L1_ffn_in['w1_w'], 'L1_ffn_w1_s': _L1_ffn_in['w1_s'], 'L1_ffn_w2_w': _L1_ffn_in['w2_w'], 'L1_ffn_w2_s': _L1_ffn_in['w2_s'], 'L1_ffn_h1_w': _L1_ffn_in['h1_w'], 'L1_ffn_h1_s': _L1_ffn_in['h1_s'], 'L1_ffn_h2_w': _L1_ffn_in['h2_w'], 'L1_ffn_h2_s': _L1_ffn_in['h2_s'], 'L1_ffn_w3_w': _L1_ffn_in['w3_w'], 'L1_ffn_w3_s': _L1_ffn_in['w3_s']}
    _x0 = _d['L0_attn_X']
    _d['L0_attn_X'] = jax.random.normal(jax.random.fold_in(jax.random.key(seed), 1), (2, 1024, 128), dtype=_x0.dtype)
    del _x0
    return _d

def reference(L0_attn_X, L0_attn_W_qkv, L0_attn_W_out, L0_ffn_norm_weight, L0_ffn_router_w, L0_ffn_sw1, L0_ffn_sb1, L0_ffn_sw2, L0_ffn_sb2, L0_ffn_ew1, L0_ffn_eb1, L0_ffn_ew2, L0_ffn_eb2, L1_attn_Wq, L1_attn_Wk, L1_attn_Wv, L1_attn_Wo, L1_attn_lambda_q1, L1_attn_lambda_k1, L1_attn_lambda_q2, L1_attn_lambda_k2, L1_attn_rms_scale, L1_ffn_w1_w, L1_ffn_w1_s, L1_ffn_w2_w, L1_ffn_w2_s, L1_ffn_h1_w, L1_ffn_h1_s, L1_ffn_h2_w, L1_ffn_h2_s, L1_ffn_w3_w, L1_ffn_w3_s):

    def _L0_attn_ref(X, W_qkv, W_out):
        import jax, jax.numpy as jnp
        import numpy as np
        D_MODEL, D_QKV, N_HEADS = (128, 64, 16)
        b, s, _ = X.shape
        h, d = (N_HEADS, D_QKV)
        scale = d ** 0.5
        qkv = X @ W_qkv
        qkv = qkv.reshape(b, s, h, d, 3)
        q, k, v = (qkv[..., 0], qkv[..., 1], qkv[..., 2])
        scores = jnp.einsum('bqhd,bkhd->bhqk', q, k) / scale
        weights = jax.nn.softmax(scores, axis=-1)
        attn = jnp.einsum('bhqk,bkhd->bqhd', weights, v)
        return attn.reshape(b, s, h * d) @ W_out

    def _L0_ffn_ref(hidden_states, norm_weight, router_w, sw1, sb1, sw2, sb2, ew1, eb1, ew2, eb2):
        import jax, jax.numpy as jnp
        import numpy as np
        D, H, O, E, TOPK = (128, 512, 128, 8, 2)
        B, S = (4, 128)
        b, s, d = hidden_states.shape
        var = jnp.mean(jnp.square(hidden_states), axis=-1, keepdims=True)
        normed = hidden_states * jax.lax.rsqrt(var + 1e-08) * norm_weight
        shared = jnp.maximum(normed @ sw1 + sb1, 0.0) @ sw2 + sb2
        flat = normed.reshape(-1, d)
        T = flat.shape[0]
        probs = jax.nn.sigmoid(flat @ router_w.T)
        scores, idx = jax.lax.top_k(probs, TOPK)
        w = scores / (jnp.sum(scores, axis=-1, keepdims=True) + 1e-06)
        comb = jnp.zeros((T, E), dtype=flat.dtype)
        comb = comb.at[jnp.arange(T)[:, None], idx].add(w)
        h = jnp.maximum(jnp.einsum('td,edh->teh', flat, ew1) + eb1[None, :, :], 0.0)
        eo = jnp.einsum('teh,eho->teo', h, ew2) + eb2[None, :, :]
        routed = jnp.einsum('teo,te->to', eo, comb)
        return shared + routed.reshape(b, s, -1)

    def _L1_attn_ref(X, Wq, Wk, Wv, Wo, lambda_q1, lambda_k1, lambda_q2, lambda_k2, rms_scale):
        import jax, jax.numpy as jnp
        import numpy as np
        import math
        NUM_HEADS = 8
        D_HEAD = 128
        DEPTH = 1
        LAMBDA_INIT = 0.8 - 0.6 * math.exp(-0.3 * DEPTH)
        EPS = 1e-05
        B, N, D = X.shape
        H, dh = (NUM_HEADS, D_HEAD)

        def proj(W):
            y = jnp.einsum('bnd,ed->bne', X, W)
            return y.reshape(B, N, H, 2 * dh).transpose(0, 2, 1, 3)
        Q = proj(Wq)
        K = proj(Wk)
        V = proj(Wv)
        Q1, Q2 = (Q[..., :dh], Q[..., dh:])
        K1, K2 = (K[..., :dh], K[..., dh:])
        lam1 = jnp.exp(jnp.sum(lambda_q1 * lambda_k1, axis=-1))
        lam2 = jnp.exp(jnp.sum(lambda_q2 * lambda_k2, axis=-1))
        lam = (lam1 - lam2 + LAMBDA_INIT)[None, :, None, None]
        scaling = 1.0 / math.sqrt(dh)
        A1 = jnp.einsum('bhqd,bhkd->bhqk', Q1, K1) * scaling
        A2 = jnp.einsum('bhqd,bhkd->bhqk', Q2, K2) * scaling
        attn = jax.nn.softmax(A1, axis=-1) - lam * jax.nn.softmax(A2, axis=-1)
        O = jnp.einsum('bhqk,bhkd->bhqd', attn, V)
        rms = jnp.sqrt(jnp.mean(O * O, axis=-1, keepdims=True) + EPS)
        O = O / rms * rms_scale
        O = O * (1.0 - LAMBDA_INIT)
        O = O.transpose(0, 2, 1, 3).reshape(B, N, H * 2 * dh)
        return jnp.einsum('bne,de->bnd', O, Wo)

    def _L1_ffn_ref(x, w1_w, w1_s, w2_w, w2_s, h1_w, h1_s, h2_w, h2_s, w3_w, w3_s):
        import jax, jax.numpy as jnp
        import numpy as np
        D_IN, D_HID = (128, 512)

        def _ternary(key, shape):
            return jax.random.randint(key, shape, -1, 2).astype(jnp.float32)

        def _tlin(x, w, s):
            return jnp.einsum('bsi,oi->bso', x, w) * s
        h = jax.nn.silu(_tlin(x, w1_w, w1_s)) * _tlin(x, w2_w, w2_s)
        h = jax.nn.gelu(_tlin(h, h1_w, h1_s), approximate=False)
        h = jax.nn.gelu(_tlin(h, h2_w, h2_s), approximate=False)
        return _tlin(h, w3_w, w3_s)
    x = L0_attn_X
    x = x + _layernorm(_L0_attn_ref(_layernorm(x, axis=-1), L0_attn_W_qkv, L0_attn_W_out), axis=-1)
    x = x + _layernorm(_L0_ffn_ref(_layernorm(x, axis=-1), L0_ffn_norm_weight, L0_ffn_router_w, L0_ffn_sw1, L0_ffn_sb1, L0_ffn_sw2, L0_ffn_sb2, L0_ffn_ew1, L0_ffn_eb1, L0_ffn_ew2, L0_ffn_eb2), axis=-1)
    x = x + _layernorm(_L1_attn_ref(_layernorm(x, axis=-1), L1_attn_Wq, L1_attn_Wk, L1_attn_Wv, L1_attn_Wo, L1_attn_lambda_q1, L1_attn_lambda_k1, L1_attn_lambda_q2, L1_attn_lambda_k2, L1_attn_rms_scale), axis=-1)
    x = x + _layernorm(_L1_ffn_ref(_layernorm(x, axis=-1), L1_ffn_w1_w, L1_ffn_w1_s, L1_ffn_w2_w, L1_ffn_w2_s, L1_ffn_h1_w, L1_ffn_h1_s, L1_ffn_h2_w, L1_ffn_h2_s, L1_ffn_w3_w, L1_ffn_w3_s), axis=-1)
    return x

_drawn_inputs = setup_inputs


def setup_inputs(seed=0):
    import zlib

    import numpy as np

    out = dict(_drawn_inputs(seed))
    spreads = {'L0_ffn_norm_weight': (1.0, 0.2),
     'L0_ffn_sb1': (0.0, 0.1),
     'L0_ffn_sb2': (0.0, 0.1),
     'L0_ffn_eb1': (0.0, 0.1),
     'L0_ffn_eb2': (0.0, 0.1),
     'L1_attn_rms_scale': (1.0, 0.2)}
    factors = {'L1_attn_Wq': 4.851,
     'L1_attn_Wk': 4.871,
     'L1_attn_lambda_q1': 8.0,
     'L1_attn_lambda_k1': 8.0,
     'L1_attn_lambda_q2': 8.0,
     'L1_attn_lambda_k2': 8.0}
    for name, (base, spread) in spreads.items():
        noise = np.random.default_rng([zlib.crc32(name.encode()), seed]).standard_normal(out[name].shape)
        drawn = base * np.exp(spread * noise) if base else spread * noise
        out[name] = jnp.asarray(drawn.astype(out[name].dtype))
    for name, factor in factors.items():
        out[name] = (out[name] * factor).astype(out[name].dtype)
    return out
```

```python
import math
from contextlib import ExitStack

import concourse.bass as bass
from concourse import mybir

F32 = mybir.dt.float32
F32R = mybir.dt.float32r
ALU = mybir.AluOpType
ACT = mybir.ActivationFunctionType
AX = mybir.AxisListType

P = 128
EPS_LN = 1e-5
EPS_RMS0 = 1e-8
EPS_TOPK = 1e-6
EPS_RMS1 = 1e-5
LAMBDA_INIT = 0.8 - 0.6 * math.exp(-0.3 * 1)
BANK = 512


def sandwich_kernel(nc, t, out):
    B, SEQ, D = t["x"].shape
    TOK = B * SEQ
    NT = TOK // P
    NC = TOK // BANK
    TPC = BANK // P
    KT = SEQ // P
    H0, DH0 = t["l0_wv"].shape[0], 64
    H1, DH1 = t["l1_w"].shape[0], 128
    DV1 = 2 * DH1
    NE = t["ffn0_w1"].shape[1]
    NR = NE - 1
    HID = t["ffn0_w1"].shape[2]
    HT = HID // P
    SLOTS = B * KT
    assert D == P and B == 2 and KT == 8 and SEQ == 2 * BANK and HT == 4

    ctx = ExitStack()
    with ctx:
        def sem(name):
            return ctx.enter_context(nc.semaphore(name))

        def sb_in(scope):
            return lambda name, shape, dt=F32: scope.enter_context(nc.sbuf_tensor(name, shape, dt))

        ps_s = ctx.enter_context(nc.psum_tensor("ps_s", [P, 2, 2, BANK], F32))
        ps_t = ctx.enter_context(nc.psum_tensor("ps_t", [P, 2, BANK], F32))
        ps_o = ctx.enter_context(nc.psum_tensor("ps_o", [P, BANK], F32))
        ps_m = ctx.enter_context(nc.psum_tensor("ps_m", [P, BANK], F32))

        sb = sb_in(ctx)
        X = sb("X", [P, NT, D])
        ident = sb("ident", [P, P])
        xT_hi = sb("xT_hi", [P, TOK], F32R)
        xT_lo = sb("xT_lo", [P, TOK], F32R)
        stats = sb("stats", [P, 2, TPC, 6])
        mv = sb("mv", [P, 2, TPC, 2])
        rstd = sb("rstd", [P, 2, TPC])
        msq = sb("msq", [P, TPC])
        r_rms = sb("r_rms", [P, TPC])
        xhat = sb("xhat", [P, TPC, D])
        xst = [sb(f"xst{i}", [P, TPC, D]) for i in range(2)]
        ones = sb("ones", [P, P])
        minus_half = sb("minus_half", [P, TPC])
        Y = sb("Y", [P, NT, D])
        Yflat = Y[:, :, :].rearrange("p t d -> p (t d)")

        scope = ExitStack()
        sb = sb_in(scope)
        xT_f = sb("xT_f", [P, TOK])
        a0_wqk_raw = sb("a0_wqk_raw", [P, 4 * DH0])
        a0_wqk_hi = sb("a0_wqk_hi", [P, 4 * DH0], F32R)
        a0_wqk_lo = sb("a0_wqk_lo", [P, 4 * DH0], F32R)
        a0_wv = sb("a0_wv", [P, 2 * DH0])
        a0_wo = sb("a0_wo", [P, D])
        a0_q = [sb(f"a0_q{b}", [P, SEQ], F32R) for b in range(B)]
        a0_kh = [sb(f"a0_kh{b}", [P, SEQ], F32R) for b in range(B)]
        a0_kl = [sb(f"a0_kl{b}", [P, SEQ], F32R) for b in range(B)]
        a0_v = [sb(f"a0_v{b}", [P, KT, 2 * DH0], F32R) for b in range(B)]
        a0_p = [sb(f"a0_p{i}", [P, SEQ]) for i in range(4)]
        a0_pth = [sb(f"a0_pth{i}", [P, KT, BANK], F32R) for i in range(2)]
        a0_ptl = [sb(f"a0_ptl{i}", [P, KT, BANK], F32R) for i in range(2)]
        a0_o = [sb(f"a0_o{i}", [P, BANK]) for i in range(2)]
        a0_negmax = sb("a0_negmax", [P, 4])
        a0_sum = sb("a0_sum", [P, 4])
        a0_rsum = sb("a0_rsum", [P, 4])
        scope.close()

        scope = ExitStack()
        sb = sb_in(scope)
        f0_w1_raw = sb("f0_w1_raw", [P, NE, HID])
        f0_w1_hi = sb("f0_w1_hi", [P, NE, HID], F32R)
        f0_w1_lo = sb("f0_w1_lo", [P, NE, HID], F32R)
        f0_w2 = sb("f0_w2", [P, NE, HT, D])
        f0_b1 = sb("f0_b1", [P, NE, HT])
        f0_b2 = sb("f0_b2", [NE, D])
        f0_nw = sb("f0_nw", [P, 1])
        f0_rw = sb("f0_rw", [P, NR])
        f0_nT = [sb(f"f0_nT{i}", [P, BANK]) for i in range(2)]
        f0_h = [[sb(f"f0_h{i}{j}", [P, BANK]) for j in range(HT)] for i in range(2)]
        f0_rank = sb("f0_rank", [P, NR])
        f0_prob = sb("f0_prob", [P, NT, NR])
        f0_left = sb("f0_left", [P, NT, NR])
        f0_tmp = sb("f0_tmp", [P, NT, NR])
        f0_tmp2 = sb("f0_tmp2", [P, NT, NR])
        f0_one = [sb(f"f0_one{i}", [P, NT, NR]) for i in range(2)]
        f0_top = [sb(f"f0_top{i}", [P, NT]) for i in range(2)]
        f0_idx = sb("f0_idx", [P, NT])
        f0_den = sb("f0_den", [P, NT])
        f0_comb = sb("f0_comb", [P, NT, NE])
        f0_combT = sb("f0_combT", [NE, TOK])
        scope.close()

        scope = ExitStack()
        sb = sb_in(scope)
        WC = 4 * DH1 + DV1
        a1_w_raw = [sb(f"a1_w_raw{b}", [P, WC]) for b in range(B)]
        a1_w_hi = [sb(f"a1_w_hi{b}", [P, WC], F32R) for b in range(B)]
        a1_w_lo = [sb(f"a1_w_lo{b}", [P, WC], F32R) for b in range(B)]
        a1_hi = [[sb(f"a1_hi{b}{j}", [P, SEQ], F32R) for j in range(4)] for b in range(B)]
        a1_lo = [[sb(f"a1_lo{b}{j}", [P, SEQ], F32R) for j in range(4)] for b in range(B)]
        a1_vh = [sb(f"a1_vh{b}", [P, KT, DV1], F32R) for b in range(B)]
        a1_vl = [sb(f"a1_vl{b}", [P, KT, DV1], F32R) for b in range(B)]
        a1_p = [[sb(f"a1_p{i}{m}", [P, SEQ]) for m in range(2)] for i in range(2)]
        a1_ath = sb("a1_ath", [P, KT, P], F32R)
        a1_atl = sb("a1_atl", [P, KT, P], F32R)
        a1_on = [sb(f"a1_on{i}", [P, DV1]) for i in range(2)]
        a1_ot = [sb(f"a1_ot{i}", [P, DV1]) for i in range(2)]
        a1_sq = sb("a1_sq", [P, DV1])
        a1_wo_raw = sb("a1_wo_raw", [P, 2, D])
        a1_wo = [sb(f"a1_wo{b}", [P, 2, D]) for b in range(B)]
        a1_rms = sb("a1_rms", [P, 2])
        a1_neglam = sb("a1_neglam", [P, H1])
        a1_lam = sb("a1_lam", [P, 4, H1])
        a1_lprod = sb("a1_lprod", [P, 2, H1])
        a1_lexp = sb("a1_lexp", [P, 2, H1])
        a1_negmax = sb("a1_negmax", [P, 2, 2])
        a1_sum = sb("a1_sum", [P, 2, 2])
        a1_rsum = sb("a1_rsum", [P, 2, 2])
        a1_c = sb("a1_c", [P, 2])
        a1_ss = sb("a1_ss", [P, 2])
        a1_r = sb("a1_r", [P, 2])
        scope.close()

        scope = ExitStack()
        sb = sb_in(scope)
        f1_raw = sb("f1_raw", [P, 2 * HID + 2 * HT * HID + HT * D])
        f1_w = sb("f1_w", [P, 2 * HID + 2 * HT * HID + HT * D], F32R)
        f1_s = sb("f1_s", [P, 4 * HT + 1])
        f1_a = [sb(f"f1_a{i}", [P, BANK]) for i in range(2)]
        f1_f = [sb(f"f1_f{i}", [P, BANK]) for i in range(2)]
        f1_hi = [[sb(f"f1_hi{i}{j}", [P, BANK], F32R) for j in range(HT)] for i in range(2)]
        f1_lo = [[sb(f"f1_lo{i}{j}", [P, BANK], F32R) for j in range(HT)] for i in range(2)]
        f1_y = [sb(f"f1_y{i}", [P, BANK]) for i in range(2)]
        scope.close()
        f1_w12 = f1_w[:, 0:2 * HID].rearrange("p (w n) -> p w n", w=2)
        f1_wh = f1_w[:, 2 * HID:2 * HID + 2 * HT * HID].rearrange("p (w k n) -> p w k n", w=2, k=HT)
        f1_w3 = f1_w[:, 2 * HID + 2 * HT * HID:].rearrange("p (k n) -> p k n", k=HT)

        x_dram = t["x"].rearrange("b (t p) d -> p (b t) d", p=P)
        out_dram = out.rearrange("b (t p) d -> p (b t) d", p=P)

        S = {name: ctx.enter_context(nc.semaphore(name)) for name in (
            "pool_step", "norm_var", "norm_rstd", "waited", "x_lo", "x_turned", "x_hi", "ident_ready", "xst_ready",
            "y_zero", "y0_used", "y0_turned", "x1_ready", "dve_step", "out_stored",
            "a0_out_added", "a0_split_lo", "a0_split_in", "a0_o_out", "a0_out_in", "a0_p_normed", "a0_pt_lo",
            "a0_turned", "a0_pv", "a0_w_lo", "a0_wv_loaded", "a0_exped", "a0_scores", "a0_wo_loaded",
            "a0_split_hi", "a0_pt_hi", "a0_negmaxed", "a0_rsummed", "a0_wqk_loaded", "a0_w_hi",
            "f0_comb_ready", "f0_combT_in", "f0_combT_ready", "f0_small_loaded", "f0_bias_in", "f0_nT_ready",
            "f0_logits", "f0_exped", "f0_w1_hi_ready", "f0_y_started", "f0_w1_lo_ready", "f0_w2_loaded",
            "f0_relued", "f0_up", "f0_added", "f0_down",
            "a1_split_in", "a1_split_hi", "a1_split_lo", "a1_exped", "a1_scores", "a1_combined", "a1_pt_lo",
            "a1_turned", "a1_o_normed", "a1_pv", "a1_added", "a1_ot_in", "a1_ot_out", "a1_out_in",
            "a1_lprod_ready", "a1_lsum_in", "a1_w_lo", "a1_lexped", "a1_wo_scaled", "a1_pt_hi", "a1_negmaxed",
            "a1_squared", "a1_lam_loaded", "a1_rsummed", "a1_c_ready", "a1_rms_ready", "a1_w_hi",
            "a1_wo_loaded", "a1_rms_loaded", "a1_rms_eps",
            "f1_loaded", "f1_w_ready", "f1_gelued", "f1_pre", "f1_split", "f1_hidden", "f1_y_out", "f1_down",
            "f1_y_used", "f1_y_turned", "f1_s_loaded", "f1_gated", "f1_silued", "f1_hi_ready",
        )}
        S["x_loaded"] = [ctx.enter_context(nc.semaphore(f"x_loaded{i}")) for i in range(NC)]
        S["f0_w1_loaded"] = [ctx.enter_context(nc.semaphore(f"f0_w1_loaded{i}")) for i in range(NE)]
        S["a1_w_loaded"] = [ctx.enter_context(nc.semaphore(f"a1_w_loaded{i}")) for i in range(B)]

        def from0(count):
            return max(count, 0) if isinstance(count, int) else count

        def row(ap, h):
            if isinstance(h, int):
                return ap[h]
            return ap[bass.ds(h, 1)].rearrange("a p n -> (a p) n")

        def heads(eng, count, body):
            body(0, True, False)
            with eng.Fori(1, count - 1) as h:
                body(h, False, False)
            body(count - 1, False, True)

        class Count:

            def __init__(self):
                self.base, self.n = 0, 0

            def next(self):
                self.n += 1
                return self.base + self.n

            def enter(self, i, per_round):
                self.start, self.per_round = self.base + self.n, per_round
                self.base, self.n = self.start + i * per_round, 0

            def leave(self, rounds):
                assert self.n == self.per_round, self.n
                self.base, self.n = self.start + rounds * self.per_round, 0

        dve_steps = Count()
        pool_steps = Count()

        NORM_IN = 0
        NORM_A0 = NORM_IN + NC
        NORM_F0 = NORM_A0 + 2 * NC
        NORM_A1 = NORM_F0 + 2 * NC
        NORM_F1 = NORM_A1 + 2 * NC

        def norm_stats(dve, n, par, src):
            for i in range(TPC):
                ins = dve.bn_stats(stats[:, par, i, :], src(i))
            ins.then_inc(S["dve_step"], 1)
            dve.wait_ge(S["dve_step"], dve_steps.next())
            dve.sem_inc(S["waited"], 1)
            for i in range(TPC):
                ins = dve.bn_aggr(mv[:, par, i, :], stats[:, par, i, :])
            ins.then_inc(S["norm_var"], 1)

        def norm_apply(dve, n, par, src, dst):
            dve.wait_ge(S["norm_rstd"], n + 1)
            for i in range(TPC):
                ins = dve.tensor_scalar(dst(i), src(i), mv[:, par, i, 0:1], rstd[:, par, i:i + 1],
                                        ALU.subtract, ALU.mult)
            return ins

        def pool_rsqrt(pool, dst, src, eps):
            pool.tensor_scalar(dst, src, eps, None, ALU.add).then_inc(S["pool_step"], 1)
            pool.wait_ge(S["pool_step"], pool_steps.next())
            pool.sem_inc(S["waited"], 1)
            return pool.tensor_tensor(dst, dst, minus_half[:, 0:dst.shape[-1]], ALU.pow)

        def norm_rstd(pool, n, par):
            pool.wait_ge(S["norm_var"], n + 1)
            pool.sem_inc(S["waited"], 1)
            pool_rsqrt(pool, rstd[:, par, :], mv[:, par, :, 1], EPS_LN).then_inc(S["norm_rstd"], 1)

        def norm_rstd_rms(pool, n, par):
            pool.wait_ge(S["norm_var"], n + 1)
            r = rstd[:, par, :]
            pool_rsqrt(pool, r, mv[:, par, :, 1], EPS_LN).then_inc(S["pool_step"], 1)
            pool.wait_ge(S["pool_step"], pool_steps.next())
            pool.sem_inc(S["waited"], 1)
            pool.tensor_tensor(msq[:, :], r, r, ALU.mult).then_inc(S["pool_step"], 1)
            pool.wait_ge(S["pool_step"], pool_steps.next())
            pool.sem_inc(S["waited"], 1)
            pool.tensor_tensor(msq[:, :], msq[:, :], mv[:, par, :, 1], ALU.mult).then_inc(S["pool_step"], 1)
            pool.wait_ge(S["pool_step"], pool_steps.next())
            pool.sem_inc(S["waited"], 1)
            pool_rsqrt(pool, r_rms[:, :], msq[:, :], EPS_RMS0).then_inc(S["pool_step"], 1)
            pool.wait_ge(S["pool_step"], pool_steps.next())
            pool.sem_inc(S["waited"], 1)
            pool.tensor_tensor(r, r, r_rms[:, :], ALU.mult).then_inc(S["norm_rstd"], 1)

        def add_and_norm(dve, n, c, src, dst):
            norm_stats(dve, n, 0, src)
            norm_apply(dve, n, 0, src, lambda i: tile(xhat, i)).then_inc(S["dve_step"], 1)
            dve.wait_ge(S["dve_step"], dve_steps.next())
            dve.sem_inc(S["waited"], 1)
            xc = X[:, bass.ds(c * TPC, TPC), :]
            dve.tensor_tensor(xc, xc, xhat[:, :, :], ALU.add).then_inc(S["dve_step"], 1)
            dve.wait_ge(S["dve_step"], dve_steps.next())
            dve.sem_inc(S["waited"], 1)
            x_tile = lambda i: X[:, bass.ds(c * TPC + i, 1), :]
            norm_stats(dve, n + 1, 1, x_tile)
            return norm_apply(dve, n + 1, 1, x_tile, dst)

        def tile(buf, i):
            return buf[:, bass.ds(i, 1), :]

        def bank_tile(bank, i):
            return bank[:, i * P:(i + 1) * P].rearrange("p (a n) -> p a n", a=1)

        TURN_IN, TURN_A0, TURN_F0, TURN_A1 = 0, NC, 2 * NC, 3 * NC

        def turn_pe(pe, k, c, src):
            pe.wait_ge(S["x_lo"], from0(k - 1))
            for i in range(TPC):
                ins = pe.transpose(ps_t[:, c % 2, i * P:(i + 1) * P], src(i), ident[:, :])
            ins.then_inc(S["x_turned"], 1)

        def turn_act(act, k, c, scale=1.0):
            act.wait_ge(S["x_turned"], k + 1)
            act.activation(xT_hi[:, c * BANK:(c + 1) * BANK], ps_t[:, c % 2, :], ACT.Copy, scale=scale)\
                .then_inc(S["x_hi"], 1)

        def turn_dve(dve, k, c, src):
            dve.wait_ge(S["x_hi"], k + 1)
            cols = slice(c * BANK, (c + 1) * BANK)
            dve.tensor_tensor(xT_lo[:, cols], src, xT_hi[:, cols], ALU.subtract).then_inc(S["x_lo"], 1)

        def input_pe(pe):
            pe.wait_ge(S["ident_ready"], 2)
            for c in range(NC):
                pe.wait_ge(S["xst_ready"], c + 1)
                turn_pe(pe, TURN_IN + c, c, lambda i: xst[c % 2][:, i, :])

        def input_act(act):
            for c in range(NC):
                act.wait_ge(S["x_turned"], c + 1)
                act.activation(xT_f[:, c * BANK:(c + 1) * BANK], ps_t[:, c % 2, :], ACT.Copy)
                turn_act(act, TURN_IN + c, c)

        def input_dve(dve):
            dve.memset(ones[:, :], 1.0)
            dve.memset(Y[:, :, :], 0.0).then_inc(S["y_zero"], 1)
            for c in range(NC):
                dve.wait_ge(S["x_loaded"][c], 16)
                x_tile = lambda i: tile(X, c * TPC + i)
                norm_stats(dve, NORM_IN + c, c % 2, x_tile)
                dve.wait_ge(S["x_turned"], from0(c - 1))
                norm_apply(dve, NORM_IN + c, c % 2, x_tile, lambda i: tile(xst[c % 2], i))\
                    .then_inc(S["xst_ready"], 1)
                if c:
                    turn_dve(dve, TURN_IN + c - 1, c - 1, ps_t[:, (c - 1) % 2, :])
            turn_dve(dve, TURN_IN + NC - 1, NC - 1, ps_t[:, (NC - 1) % 2, :])

        def input_pool(pool):
            pool.memset(minus_half[:, :], -0.5).then_inc(S["pool_step"], 1)
            pool.wait_ge(S["pool_step"], pool_steps.next())
            pool.sem_inc(S["waited"], 1)
            pool.memset(ident[:, :], 0.0).then_inc(S["ident_ready"], 1)
            pool.wait_ge(S["ident_ready"], 1)
            pool.affine_select(out=ident[:, :], in_=ident[:, :], compare_op=ALU.not_equal, fill=1.0, base=0,
                               pattern=[[-1, P]], channel_multiplier=1).then_inc(S["ident_ready"], 1)
            for c in range(NC):
                norm_rstd(pool, NORM_IN + c, c % 2)

        def input_sp(sp):
            for c in range(NC):
                sp.dma_start(X[:, c * TPC:(c + 1) * TPC, :], x_dram[:, c * TPC:(c + 1) * TPC, :])\
                    .then_inc(S["x_loaded"][c], 16)
                if c == 0:
                    a0_load_first(sp)

        A0_PIECES = {
            0: ("k", 1, 0), 1: ("k", 1, 1), 2: ("q", 1, 0), 3: ("out", -2), 4: ("v", 0, 0), 5: ("v", 0, 1),
            6: ("q", 1, 1), 7: ("out", -1), 8: ("v", 1, 0), 9: ("k", 0, 0), 10: ("k", 0, 1), 11: ("out", 0),
            12: ("v", 1, 1), 13: ("q", 0, 0), 14: ("q", 0, 1), 15: ("out", 1)}
        A0_NEXT = (9, 10, 13, 14)
        A0_SPLITS = [s for s in range(SLOTS) if A0_PIECES[s][0] != "out"]

        def a0_piece(s, first, last):
            piece = A0_PIECES[s]
            if (first and piece[0] == "out" and piece[1] < 0) or (last and s in A0_NEXT):
                return None
            return piece

        def a0_splits(h, s, last):
            n = sum(1 for z in A0_SPLITS if z <= s and not (last and z in A0_NEXT))
            return h * len(A0_SPLITS) + (len(A0_NEXT) + n)

        def a0_outs(h, s):
            return h * 4 + (sum(1 for z in range(s + 1) if A0_PIECES[z][0] == "out") - 2)

        def a0_bank_free(pe, h, s, first, last):
            z = s - 1
            while z >= 0 and a0_piece(z, first, last) is None:
                z -= 1
            if (z >= 0 and A0_PIECES[z][0] == "out") or (z < 0 and not first):
                pe.wait_ge(S["a0_out_added"], a0_outs(h, z))
            else:
                pe.wait_ge(S["a0_split_lo"], a0_splits(h, z, last))

        def a0_pe_split(pe, piece):
            kind, b, half = piece
            if kind == "v":
                for j in range(TPC):
                    k0 = b * SEQ + half * BANK + j * P
                    ins = pe.matmul(ps_m[:, j * P:(j + 1) * P], xT_f[:, k0:k0 + P], a0_wv[:, :], start=True, stop=True)
            else:
                w = slice(0, 2 * DH0) if kind == "q" else slice(2 * DH0, 4 * DH0)
                x = slice(b * SEQ + half * BANK, b * SEQ + (half + 1) * BANK)
                pe.matmul(ps_m[:, :], a0_wqk_hi[:, w], xT_hi[:, x], start=True, stop=False)
                pe.matmul(ps_m[:, :], a0_wqk_hi[:, w], xT_lo[:, x], start=False, stop=False)
                ins = pe.matmul(ps_m[:, :], a0_wqk_lo[:, w], xT_hi[:, x], start=False, stop=True)
            ins.then_inc(S["a0_split_in"], 1)

        def a0_pe_out(pe, n, par):
            pe.wait_ge(S["a0_o_out"], n + 1)
            pe.matmul(ps_m[:, :], a0_wo[:, :], a0_o[par][:, :], start=True, stop=True).then_inc(S["a0_out_in"], 1)

        def a0_pe_turn(pe, g, q):
            pe.wait_ge(S["a0_p_normed"], g + 1)
            for half in range(2):
                pe.wait_ge(S["a0_pt_lo"], from0(2 * g + (half - 1)))
                for j in range(4):
                    k0 = (half * 4 + j) * P
                    ins = pe.transpose(ps_t[:, half, j * P:(j + 1) * P], a0_p[q % 4][:, k0:k0 + P], ident[:, :])
                ins.then_inc(S["a0_turned"], 1)

        def a0_pe_pv(pe, n, of_head, quarter):
            if quarter == 0:
                pe.wait_ge(S["a0_pt_lo"], 8 * n + 8)
                pe.wait_ge(S["a0_o_out"], n)
            b, par = of_head // 2, of_head % 2
            for kt in range(2 * quarter, 2 * quarter + 2):
                pe.matmul(ps_o[:, :], a0_v[b][:, kt, :], a0_pth[par][:, kt, :], start=kt == 0, stop=False)
                ins = pe.matmul(ps_o[:, :], a0_v[b][:, kt, :], a0_ptl[par][:, kt, :], start=False, stop=kt == KT - 1)
            if quarter == 3:
                ins.then_inc(S["a0_pv"], 1)

        def a0_pe(pe):
            pe.wait_ge(S["x_lo"], NC)
            pe.wait_ge(S["a0_w_lo"], 1)
            for i, s in enumerate(A0_NEXT):
                pe.wait_ge(S["a0_split_lo"], i)
                a0_pe_split(pe, A0_PIECES[s])
            pe.wait_ge(S["a0_wv_loaded"], 16)

            def body(h, first, last):
                for s in range(SLOTS):
                    g = h * SLOTS + s
                    b, q = s // KT, s % KT
                    if s in (0, KT):
                        pe.wait_ge(S["a0_split_lo"], a0_splits(h, s - 1, last))
                    pe.wait_ge(S["a0_exped"], from0(g - 1))
                    for half in range(2):
                        k = slice(half * BANK, (half + 1) * BANK)
                        queries = a0_q[b][:, q * P:(q + 1) * P]
                        pe.matmul(ps_s[:, s % 2, half, :], queries, a0_kh[b][:, k], start=True, stop=False)
                        ins = pe.matmul(ps_s[:, s % 2, half, :], queries, a0_kl[b][:, k], start=False, stop=True)
                    ins.then_inc(S["a0_scores"], 1)
                    piece = a0_piece(s, first, last)
                    if piece is not None:
                        a0_bank_free(pe, h, s, first, last)
                        if piece[0] == "out":
                            if s == 11:
                                pe.wait_ge(S["a0_wo_loaded"], h * 16 + 16)
                            a0_pe_out(pe, h * 4 + piece[1], piece[1] % 2)
                        else:
                            if s == 4:
                                pe.wait_ge(S["a0_wv_loaded"], h * 16 + 16)
                            if s == A0_NEXT[0]:
                                pe.wait_ge(S["a0_w_lo"], h + 2)
                            a0_pe_split(pe, piece)
                    if not (first and s < 2):
                        a0_pe_turn(pe, g - 2, (s - 2) % SLOTS)
                    n, quarter = (s - 6) // 4, (s - 6) % 4
                    if not (first and n < 0):
                        if s in (6, 14):
                            pe.wait_ge(S["a0_split_lo"], a0_splits(h, s - 1, last))
                        a0_pe_pv(pe, h * 4 + n, n % 4, quarter)

            heads(pe, H0, body)
            g, n = H0 * SLOTS, H0 * 4
            for i in range(2):
                a0_pe_turn(pe, g - 2 + i, SLOTS - 2 + i)
                a0_pe_pv(pe, n - 2, 2, 2 + i)
            for quarter in range(4):
                a0_pe_pv(pe, n - 1, 3, quarter)
                if quarter == 1:
                    pe.wait_ge(S["a0_out_added"], n - 2)
                    a0_pe_out(pe, n - 2, 0)
            pe.wait_ge(S["a0_out_added"], n - 1)
            a0_pe_out(pe, n - 1, 1)

        def a0_act_split(act, count, piece):
            kind, b, half = piece
            cols = slice(half * BANK, (half + 1) * BANK)
            act.wait_ge(S["a0_split_in"], count)
            if kind == "v":
                src = ps_m[:, :].rearrange("p (t c) -> p t c", c=P)[:, :, 0:DH0]
                ins = act.activation(a0_v[b][:, half * TPC:(half + 1) * TPC, 0:DH0], src, ACT.Copy)
            elif kind == "q":
                ins = act.activation(a0_q[b][:, cols], ps_m[:, :], ACT.Copy, scale=DH0 ** -0.5)
            else:
                ins = act.activation(a0_kh[b][:, cols], ps_m[:, :], ACT.Copy)
            ins.then_inc(S["a0_split_hi"], 1)

        def a0_dve_split(dve, count, piece):
            kind, b, half = piece
            cols = slice(half * BANK, (half + 1) * BANK)
            dve.wait_ge(S["a0_split_hi"], count)
            if kind == "v":
                src = ps_m[:, :].rearrange("p (t c) -> p t c", c=P)[:, :, DH0:2 * DH0]
                v = a0_v[b][:, half * TPC:(half + 1) * TPC, :]
                ins = dve.tensor_tensor(v[:, :, DH0:2 * DH0], src, v[:, :, 0:DH0], ALU.subtract)
            elif kind == "q":
                low = a0_q[b][DH0:2 * DH0, cols]
                ins = dve.scalar_tensor_tensor(out=low, in0=ps_m[DH0:2 * DH0, :], scalar=DH0 ** -0.5, in1=low,
                                               op0=ALU.mult, op1=ALU.subtract)
            else:
                ins = dve.tensor_tensor(a0_kl[b][:, cols], ps_m[:, :], a0_kh[b][:, cols], ALU.subtract)
            ins.then_inc(S["a0_split_lo"], 1)

        def a0_pt_part(q, half):
            return slice(None), slice(half * 4, half * 4 + 4), slice((q % 4) * P, (q % 4 + 1) * P)

        def a0_act(act):
            for i, s in enumerate(A0_NEXT):
                a0_act_split(act, i + 1, A0_PIECES[s])

            def pt_hi(g, q):
                for half in range(2):
                    act.wait_ge(S["a0_turned"], 2 * g + (half + 1))
                    act.activation(a0_pth[(q // 4) % 2][a0_pt_part(q, half)],
                                   ps_t[:, half, :].rearrange("p (t c) -> p t c", c=P), ACT.Copy)\
                        .then_inc(S["a0_pt_hi"], 1)

            def o_out(n, par):
                act.wait_ge(S["a0_pv"], n + 1)
                act.wait_ge(S["a0_out_in"], from0(n - 1))
                act.activation(a0_o[par][:, :], ps_o[:, :], ACT.Copy).then_inc(S["a0_o_out"], 1)

            def body(h, first, last):
                for s in range(SLOTS):
                    g = h * SLOTS + s
                    if s % 4 == 2 and not (first and s < 10):
                        o_out(h * 4 + (s - 10) // 4, (s - 10) // 4 % 2)
                    piece = a0_piece(s, first, last)
                    if piece is not None and piece[0] != "out":
                        a0_act_split(act, a0_splits(h, s, last), piece)
                    if not (first and s < 2):
                        q = (s - 2) % SLOTS
                        if q % 4 == 0:
                            act.wait_ge(S["a0_pv"], from0(h * 4 + ((s - 2) // 4 - 1)))
                        pt_hi(g - 2, q)
                    act.wait_ge(S["a0_negmaxed"], g + 1)
                    act.wait_ge(S["a0_turned"], from0(2 * g - 6))
                    act.activation(a0_p[s % 4][:, :], ps_s[:, s % 2, :, :], ACT.Exp, bias=a0_negmax[:, s % 4:s % 4 + 1],
                                   accum_out=a0_sum[:, s % 4:s % 4 + 1]).then_inc(S["a0_exped"], 1)

            heads(act, H0, body)
            g, n = H0 * SLOTS, H0 * 4
            pt_hi(g - 2, SLOTS - 2)
            pt_hi(g - 1, SLOTS - 1)
            o_out(n - 2, 0)
            o_out(n - 1, 1)

        def a0_dve(dve):
            for i, s in enumerate(A0_NEXT):
                a0_dve_split(dve, i + 1, A0_PIECES[s])

            def pt_lo(g, q):
                for half in range(2):
                    dve.wait_ge(S["a0_pt_hi"], 2 * g + (half + 1))
                    at = a0_pt_part(q, half)
                    dve.tensor_tensor(a0_ptl[(q // 4) % 2][at], ps_t[:, half, :].rearrange("p (t c) -> p t c", c=P),
                                      a0_pth[(q // 4) % 2][at], ALU.subtract).then_inc(S["a0_pt_lo"], 1)

            def add_out(n, of_head):
                dve.wait_ge(S["a0_out_in"], n + 1)
                dve.wait_ge(S["a0_out_added"], n)
                y = Yflat[:, of_head * BANK:(of_head + 1) * BANK]
                dve.tensor_tensor(y, ps_m[:, :], y, ALU.add).then_inc(S["a0_out_added"], 1)

            def rsum(g, s):
                col = slice(s % 4, s % 4 + 1)
                dve.wait_ge(S["a0_exped"], g + 1)
                dve.wait_ge(S["a0_p_normed"], from0(g - 3))
                dve.reciprocal(a0_rsum[:, col], a0_sum[:, col]).then_inc(S["a0_rsummed"], 1)

            def body(h, first, last):
                for s in range(SLOTS):
                    g = h * SLOTS + s
                    dve.wait_ge(S["a0_scores"], g + 1)
                    dve.tensor_reduce(a0_negmax[:, s % 4:s % 4 + 1], ps_s[:, s % 2, :, :], AX.XY, ALU.max, negate=True)\
                        .then_inc(S["a0_negmaxed"], 1)
                    if not (first and s < 1):
                        rsum(g - 1, (s - 1) % SLOTS)
                    piece = a0_piece(s, first, last)
                    if piece is not None and piece[0] == "out":
                        add_out(h * 4 + piece[1], piece[1] % 4)
                    elif piece is not None:
                        a0_dve_split(dve, a0_splits(h, s, last), piece)
                    if not (first and s < 2):
                        pt_lo(g - 2, (s - 2) % SLOTS)

            heads(dve, H0, body)
            g, n = H0 * SLOTS, H0 * 4
            rsum(g - 1, SLOTS - 1)
            pt_lo(g - 2, SLOTS - 2)
            pt_lo(g - 1, SLOTS - 1)
            add_out(n - 2, 2)
            add_out(n - 1, 3)

        def a0_pool(pool):
            def weights(h):
                pool.wait_ge(S["a0_wqk_loaded"], h * 16 + 16)
                pool.sem_inc(S["waited"], 1)
                pool.tensor_scalar(a0_wqk_hi[:, :], a0_wqk_raw[:, :], 1.0, 0.0, ALU.mult, ALU.add)\
                    .then_inc(S["a0_w_hi"], 1)
                pool.wait_ge(S["a0_w_hi"], h + 1)
                pool.tensor_tensor(a0_wqk_lo[:, :], a0_wqk_raw[:, :], a0_wqk_hi[:, :], ALU.subtract)\
                    .then_inc(S["a0_w_lo"], 1)

            weights(0)

            def scale(g, s):
                pool.wait_ge(S["a0_rsummed"], g + 1)
                pool.sem_inc(S["waited"], 1)
                pool.tensor_scalar(a0_p[s % 4][:, :], a0_p[s % 4][:, :], a0_rsum[:, s % 4:s % 4 + 1], 1.0,
                                   ALU.mult, ALU.mult).then_inc(S["a0_p_normed"], 1)

            def body(h, first, last):
                for s in range(SLOTS):
                    g = h * SLOTS + s
                    if s == 7 and not last:
                        pool.wait_ge(S["a0_split_in"], a0_splits(h, 6, last))
                        weights(h + 1)
                    if not (first and s < 1):
                        scale(g - 1, (s - 1) % SLOTS)

            heads(pool, H0, body)
            scale(H0 * SLOTS - 1, SLOTS - 1)

        def a0_load_first(sp):
            sp.dma_start(a0_wqk_raw[:, :], t["l0_wqk"][0]).then_inc(S["a0_wqk_loaded"], 16)
            sp.dma_start(a0_wv[:, :], t["l0_wv"][0]).then_inc(S["a0_wv_loaded"], 16)

        def a0_sp(sp):
            def body(h, first, last):
                if not last:
                    sp.wait_ge(S["a0_w_lo"], h + 1)
                    sp.dma_start(a0_wqk_raw[:, :], row(t["l0_wqk"], h + 1)).then_inc(S["a0_wqk_loaded"], 16)
                sp.wait_ge(S["a0_out_in"], h * 4)
                sp.dma_start(a0_wo[:, :], row(t["l0_wo"], h)).then_inc(S["a0_wo_loaded"], 16)
                if not last:
                    sp.wait_ge(S["a0_split_in"], a0_splits(h, 12, last))
                    sp.dma_start(a0_wv[:, :], row(t["l0_wv"], h + 1)).then_inc(S["a0_wv_loaded"], 16)

            heads(sp, H0, body)

        def f0_pre_pe(pe):
            pe.wait_ge(S["a0_out_added"], 4 * H0)
            for c in range(NC):
                pe.wait_ge(S["y0_used"], c)
                for i in range(TPC):
                    ins = pe.transpose(ps_o[:, i * P:(i + 1) * P], Yflat[:, (c * TPC + i) * P:(c * TPC + i + 1) * P],
                                       ident[:, :])
                ins.then_inc(S["y0_turned"], 1)
                if c:
                    logits_pe(pe, c - 1)
                pe.wait_ge(S["xst_ready"], NC + c + 1)
                turn_pe(pe, TURN_A0 + c, c, lambda i: xst[c % 2][:, i, :])
            logits_pe(pe, NC - 1)
            pe.wait_ge(S["f0_comb_ready"], 1)
            for i in range(NT):
                ins = pe.transpose(ps_s[0:NE, i // 8, i // 4 % 2, (i % 4) * P:(i % 4 + 1) * P], f0_comb[:, i, :],
                                   ident[:, :])
            ins.then_inc(S["f0_combT_in"], 1)
            pe.wait_ge(S["f0_combT_ready"], 1)
            pe.wait_ge(S["f0_small_loaded"], 16 * 4)
            for i in range(NT):
                ins = pe.matmul(ps_s[:, i // 8, i // 4 % 2, (i % 4) * P:(i % 4 + 1) * P],
                                f0_combT[:, i * P:(i + 1) * P], f0_b2[:, :], start=True, stop=True)
            ins.then_inc(S["f0_bias_in"], 1)

        def logits_pe(pe, c):
            pe.wait_ge(S["f0_nT_ready"], c + 1)
            for i in range(TPC):
                k = (c * TPC + i) * NR
                ins = pe.matmul(ps_m[:, k:k + NR], f0_nT[c % 2][:, i * P:(i + 1) * P], f0_rw[:, :], start=True, stop=True)
            ins.then_inc(S["f0_logits"], 1)

        def f0_pre_act(act):
            act.wait_ge(S["f0_small_loaded"], 16 * 4)
            for c in range(NC):
                act.wait_ge(S["x_turned"], TURN_A0 + c + 1)
                act.wait_ge(S["f0_logits"], from0(c - 1))
                act.activation(f0_nT[c % 2][:, :], ps_t[:, c % 2, :], ACT.Copy, scale=f0_nw[:, 0:1])\
                    .then_inc(S["f0_nT_ready"], 1)
                turn_act(act, TURN_A0 + c, c, scale=f0_nw[:, 0:1])
            act.wait_ge(S["f0_logits"], NC)
            act.activation(f0_prob[:, :, :], ps_m[:, 0:NT * NR].rearrange("p (t e) -> p t e", e=NR), ACT.Exp,
                           scale=-1.0).then_inc(S["f0_exped"], 1)
            for e in range(NE):
                act.wait_ge(S["f0_w1_loaded"][e], 16)
                act.activation(f0_w1_hi[:, e, :], f0_w1_raw[:, e, :], ACT.Copy).then_inc(S["f0_w1_hi_ready"], 1)
            act.wait_ge(S["f0_combT_in"], 1)
            act.activation(f0_combT[:, :], ps_s[0:NE, :, :, :], ACT.Copy).then_inc(S["f0_combT_ready"], 1)
            act.wait_ge(S["f0_bias_in"], 1)
            act.activation(Y[:, :, :], ps_s[:, :, :, :], ACT.Copy).then_inc(S["f0_y_started"], 1)

        def f0_pre_dve(dve):
            for e in range(NR):
                ins = dve.memset(f0_rank[:, e:e + 1], float(NR - e))
            ins.then_inc(S["dve_step"], 1)
            dve.wait_ge(S["dve_step"], dve_steps.next())
            dve.sem_inc(S["waited"], 1)
            for c in range(NC):
                dve.wait_ge(S["y0_turned"], c + 1)
                dve.wait_ge(S["x_turned"], from0(TURN_A0 + c - 1))
                n = NORM_A0 + 2 * c
                src = lambda i: bank_tile(ps_o, i)
                norm_stats(dve, n, 0, src)
                ins = norm_apply(dve, n, 0, src, lambda i: tile(xhat, i))
                ins.then_inc(S["y0_used"], 1)
                dve.wait_ge(S["y0_used"], c + 1)
                xc = X[:, c * TPC:(c + 1) * TPC, :]
                dve.tensor_tensor(xc, xc, xhat[:, :, :], ALU.add).then_inc(S["dve_step"], 1)
                dve.wait_ge(S["dve_step"], dve_steps.next())
                dve.sem_inc(S["waited"], 1)
                x_tile = lambda i: tile(X, c * TPC + i)
                norm_stats(dve, n + 1, 1, x_tile)
                if c:
                    turn_dve(dve, TURN_A0 + c - 1, c - 1, f0_nT[(c - 1) % 2][:, :])
                norm_apply(dve, n + 1, 1, x_tile, lambda i: tile(xst[c % 2], i)).then_inc(S["xst_ready"], 1)
            turn_dve(dve, TURN_A0 + NC - 1, NC - 1, f0_nT[(NC - 1) % 2][:, :])

            def step(ins):
                ins.then_inc(S["dve_step"], 1)
                dve.wait_ge(S["dve_step"], dve_steps.next())

            over_e = lambda ap: ap[:, :].rearrange("p (t a) -> p t a", a=1).broadcast_to([P, NT, NR])
            rank = f0_rank[:, :].rearrange("p (a e) -> p a e", a=1).broadcast_to([P, NT, NR])
            dve.wait_ge(S["f0_exped"], 1)
            step(dve.tensor_scalar(f0_tmp[:, :, :], f0_prob[:, :, :], 1.0, None, ALU.add))
            step(dve.reciprocal(f0_prob[:, :, :], f0_tmp[:, :, :]))
            for k, p in ((0, f0_prob), (1, f0_left)):
                step(dve.tensor_reduce(f0_top[k][:, :], p[:, :, :], AX.X, ALU.max))
                step(dve.tensor_tensor(f0_tmp[:, :, :], p[:, :, :], over_e(f0_top[k]), ALU.is_equal))
                step(dve.tensor_tensor(f0_tmp2[:, :, :], f0_tmp[:, :, :], rank, ALU.mult))
                step(dve.tensor_reduce(f0_idx[:, :], f0_tmp2[:, :, :], AX.X, ALU.max))
                step(dve.tensor_tensor(f0_one[k][:, :, :], f0_tmp2[:, :, :], over_e(f0_idx), ALU.is_equal))
                if k == 0:
                    step(dve.scalar_tensor_tensor(out=f0_left[:, :, :], in0=f0_one[0][:, :, :], scalar=-4.0,
                                                  in1=f0_prob[:, :, :], op0=ALU.mult, op1=ALU.add))
            step(dve.tensor_tensor(f0_den[:, :], f0_top[0][:, :], f0_top[1][:, :], ALU.add))
            step(dve.tensor_scalar(f0_den[:, :], f0_den[:, :], EPS_TOPK, None, ALU.add))
            step(dve.reciprocal(f0_idx[:, :], f0_den[:, :]))
            for k in range(2):
                step(dve.tensor_tensor(f0_top[k][:, :], f0_top[k][:, :], f0_idx[:, :], ALU.mult))
                step(dve.tensor_tensor(f0_one[k][:, :, :], f0_one[k][:, :, :], over_e(f0_top[k]), ALU.mult))
            dve.memset(f0_comb[:, :, NR:NE], 1.0)
            dve.tensor_tensor(f0_comb[:, :, 0:NR], f0_one[0][:, :, :], f0_one[1][:, :, :], ALU.add)\
                .then_inc(S["f0_comb_ready"], 1)
            for e in range(NE):
                dve.wait_ge(S["f0_w1_hi_ready"], e + 1)
                dve.tensor_tensor(f0_w1_lo[:, e, :], f0_w1_raw[:, e, :], f0_w1_hi[:, e, :], ALU.subtract)\
                    .then_inc(S["f0_w1_lo_ready"], 1)

        def f0_pre_pool(pool):
            for c in range(NC):
                norm_rstd(pool, NORM_A0 + 2 * c, 0)
                norm_rstd_rms(pool, NORM_A0 + 2 * c + 1, 1)

        def f0_sp(sp):
            sp.wait_ge(S["a0_out_added"], 4 * H0)
            for dst, name in ((f0_rw, "ffn0_rw"), (f0_nw, "ffn0_nw"), (f0_b2, "ffn0_b2")):
                sp.dma_start(dst[:, :], t[name]).then_inc(S["f0_small_loaded"], 16)
            sp.dma_start(f0_b1[:, :, :], t["ffn0_b1"]).then_inc(S["f0_small_loaded"], 16)
            for e in range(NE):
                sp.dma_start(f0_w1_raw[:, e, :], t["ffn0_w1"][:, e, :]).then_inc(S["f0_w1_loaded"][e], 16)
            sp.dma_start(f0_w2[:, :, :, :], t["ffn0_w2"]).then_inc(S["f0_w2_loaded"], 16)

        def f0_pe(pe):
            pe.wait_ge(S["f0_w1_lo_ready"], NE)
            pe.wait_ge(S["f0_w2_loaded"], 16)
            pe.wait_ge(S["x_lo"], TURN_F0)
            pe.wait_ge(S["f0_y_started"], 1)
            with pe.Fori(0, NC) as c:
                x = bass.ds(c * BANK, BANK)

                def up(e):
                    for ht in range(HT):
                        if e == 0:
                            pe.wait_ge(S["f0_relued"], c * (NE * HT))
                        else:
                            pe.wait_ge(S["f0_relued"], from0(c * (NE * HT) + (HT * e + ht - 3)))
                        bank = ps_s[:, ht // 2, ht % 2, :]
                        w = slice(ht * P, (ht + 1) * P)
                        pe.matmul(bank, f0_w1_hi[:, e, w], xT_hi[:, x], start=True, stop=False)
                        pe.matmul(bank, f0_w1_hi[:, e, w], xT_lo[:, x], start=False, stop=False)
                        pe.matmul(bank, f0_w1_lo[:, e, w], xT_hi[:, x], start=False, stop=True)\
                            .then_inc(S["f0_up"], 1)

                def down(e):
                    pe.wait_ge(S["f0_relued"], c * (NE * HT) + HT * (e + 1))
                    pe.wait_ge(S["f0_added"], from0(c * NE + max(e - 1, 0)))
                    for i in range(TPC):
                        for ht in range(HT):
                            ins = pe.matmul(ps_t[:, e % 2, i * P:(i + 1) * P], f0_h[e % 2][ht][:, i * P:(i + 1) * P],
                                            f0_w2[:, e, ht, :], start=ht == 0, stop=ht == HT - 1)
                    ins.then_inc(S["f0_down"], 1)

                for e in range(NE):
                    up(e)
                    if e:
                        down(e - 1)
                down(NE - 1)

        def f0_act(act):
            with act.Fori(0, NC) as c:
                for e in range(NE):
                    for ht in range(HT):
                        act.wait_ge(S["f0_up"], c * (NE * HT) + (HT * e + ht + 1))
                        if ht == 0:
                            act.wait_ge(S["f0_down"], from0(c * NE + max(e - 1, 0)))
                        act.activation(f0_h[e % 2][ht][:, :], ps_s[:, ht // 2, ht % 2, :], ACT.Relu,
                                       bias=f0_b1[:, e, ht:ht + 1]).then_inc(S["f0_relued"], 1)

        def f0_dve(dve):
            dve.wait_ge(S["f0_y_started"], 1)
            with dve.Fori(0, NC) as c:
                dve_steps.enter(c, 4)
                for e in range(NE):
                    dve.wait_ge(S["f0_down"], c * NE + (e + 1))
                    dve.wait_ge(S["f0_added"], c * NE + e)
                    for i in range(TPC):
                        y = Y[:, bass.ds(c * TPC + i, 1), :]
                        w = f0_comb[:, bass.ds(c * TPC + i, 1), e:e + 1].rearrange("p a b -> p (a b)")
                        ins = dve.scalar_tensor_tensor(out=y, in0=bank_tile(ps_t[:, e % 2, :], i), scalar=w, in1=y,
                                                       op0=ALU.mult, op1=ALU.add)
                    ins.then_inc(S["f0_added"], 1)
                dve.wait_ge(S["f0_added"], c * NE + NE)
                dve.sem_inc(S["waited"], 1)
                y_tile = lambda i: Y[:, bass.ds(c * TPC + i, 1), :]
                add_and_norm(dve, c * 2 + NORM_F0, c, y_tile, y_tile).then_inc(S["x1_ready"], 1)
                dve_steps.leave(NC)

        def f0_pool(pool):
            with pool.Fori(0, NC) as c:
                pool_steps.enter(c, 2)
                norm_rstd(pool, c * 2 + NORM_F0, 0)
                norm_rstd(pool, c * 2 + (NORM_F0 + 1), 1)
                pool_steps.leave(NC)

        Q1, Q2, K1, K2, V = range(5)
        HALF_BODY = [[(K1, 0)], [(K1, 1), (V, 0)], [(Q1, 0), (V, 1)], [(Q1, 1), (V, 2)],
                     [(K2, 0), (V, 3)], [(K2, 1)], [(Q2, 0)], [(Q2, 1)]]
        A1_FIRST = [piece for slot in HALF_BODY for piece in slot]
        NP1 = len(A1_FIRST)

        def a1_pieces(s, last):
            if last and s >= KT:
                return []
            return [(kind, 1 if s < KT else 0, half) for kind, half in HALF_BODY[s % KT]]

        def a1_splits(h, s, last, of_slot=99):
            n = sum(len(a1_pieces(z, last)) for z in range(s)) + min(of_slot, len(a1_pieces(s, last)) if s >= 0 else 0)
            return h * (2 * NP1) + (NP1 + n)

        def a1_pe_piece(pe, piece):
            kind, b, half = piece
            if kind == V:
                w = slice(4 * DH1, 4 * DH1 + DV1)
                for j in range(2):
                    k0 = b * SEQ + (half * 2 + j) * P
                    dst = ps_m[:, j * DV1:(j + 1) * DV1]
                    pe.matmul(dst, xT_hi[:, k0:k0 + P], a1_w_hi[b][:, w], start=True, stop=False)
                    pe.matmul(dst, xT_hi[:, k0:k0 + P], a1_w_lo[b][:, w], start=False, stop=False)
                    ins = pe.matmul(dst, xT_lo[:, k0:k0 + P], a1_w_hi[b][:, w], start=False, stop=True)
            else:
                w = slice(kind * DH1, (kind + 1) * DH1)
                x = slice(b * SEQ + half * BANK, b * SEQ + (half + 1) * BANK)
                pe.matmul(ps_m[:, :], a1_w_hi[b][:, w], xT_hi[:, x], start=True, stop=False)
                pe.matmul(ps_m[:, :], a1_w_hi[b][:, w], xT_lo[:, x], start=False, stop=False)
                ins = pe.matmul(ps_m[:, :], a1_w_lo[b][:, w], xT_hi[:, x], start=False, stop=True)
            ins.then_inc(S["a1_split_in"], 1)

        def a1_piece_parts(piece):
            kind, b, half = piece
            if kind == V:
                tiles = slice(2 * half, 2 * half + 2)
                return (a1_vh[b][:, tiles, :], a1_vl[b][:, tiles, :],
                        ps_m[:, :].rearrange("p (t c) -> p t c", t=2), 1.0)
            cols = slice(half * BANK, (half + 1) * BANK)
            return (a1_hi[b][kind][:, cols], a1_lo[b][kind][:, cols], ps_m[:, :],
                    DH1 ** -0.5 if kind in (Q1, Q2) else 1.0)

        def a1_act_piece(act, count, piece):
            hi, lo, src, scale = a1_piece_parts(piece)
            act.wait_ge(S["a1_split_in"], count)
            act.activation(hi, src, ACT.Copy, scale=scale).then_inc(S["a1_split_hi"], 1)

        def a1_dve_piece(dve, count, piece):
            hi, lo, src, scale = a1_piece_parts(piece)
            dve.wait_ge(S["a1_split_hi"], count)
            if scale == 1.0:
                ins = dve.tensor_tensor(lo, src, hi, ALU.subtract)
            else:
                ins = dve.scalar_tensor_tensor(out=lo, in0=src, scalar=scale, in1=hi, op0=ALU.mult, op1=ALU.subtract)
            ins.then_inc(S["a1_split_lo"], 1)

        def a1_pe_scores(pe, g, b, q, m):
            pe.wait_ge(S["a1_exped"], from0(2 * g + (m - 1)))
            for half in range(2):
                k = slice(half * BANK, (half + 1) * BANK)
                qs = slice(q * P, (q + 1) * P)
                dst = ps_s[:, m, half, :]
                pe.matmul(dst, a1_hi[b][Q1 + m][:, qs], a1_hi[b][K1 + m][:, k], start=True, stop=False)
                pe.matmul(dst, a1_hi[b][Q1 + m][:, qs], a1_lo[b][K1 + m][:, k], start=False, stop=False)
                ins = pe.matmul(dst, a1_lo[b][Q1 + m][:, qs], a1_hi[b][K1 + m][:, k], start=False, stop=True)
            ins.then_inc(S["a1_scores"], 1)

        def a1_pe_turn(pe, g, par):
            pe.wait_ge(S["a1_combined"], g + 1)
            for half in range(2):
                pe.wait_ge(S["a1_pt_lo"], from0(2 * g + (half - 1)))
                for j in range(4):
                    k0 = (half * 4 + j) * P
                    ins = pe.transpose(ps_t[:, half, j * P:(j + 1) * P], a1_p[par][0][:, k0:k0 + P], ident[:, :])
                ins.then_inc(S["a1_turned"], 1)

        def a1_pe_pv(pe, g, b, half):
            if half == 0:
                pe.wait_ge(S["a1_o_normed"], g)
            pe.wait_ge(S["a1_pt_lo"], 2 * g + (half + 1))
            dst = ps_o[:, 0:DV1]
            for kt in range(4 * half, 4 * half + 4):
                pe.matmul(dst, a1_ath[:, kt, :], a1_vh[b][:, kt, :], start=kt == 0, stop=False)
                pe.matmul(dst, a1_ath[:, kt, :], a1_vl[b][:, kt, :], start=False, stop=False)
                ins = pe.matmul(dst, a1_atl[:, kt, :], a1_vh[b][:, kt, :], start=False, stop=kt == KT - 1)
            if half == 1:
                ins.then_inc(S["a1_pv"], 1)

        def a1_pe_turn_o(pe, g, par):
            pe.wait_ge(S["a1_o_normed"], g + 1)
            pe.wait_ge(S["a1_added"], g)
            for j in range(2):
                ins = pe.transpose(ps_m[:, j * P:(j + 1) * P], a1_on[par][:, j * P:(j + 1) * P], ident[:, :])
            ins.then_inc(S["a1_ot_in"], 1)

        def a1_pe_out(pe, g, par, b):
            pe.wait_ge(S["a1_ot_out"], g + 1)
            for j in range(2):
                ins = pe.matmul(ps_m[:, 2 * P:3 * P], a1_ot[par][:, j * P:(j + 1) * P], a1_wo[b][:, j, :],
                                start=j == 0, stop=j == 1)
            ins.then_inc(S["a1_out_in"], 1)

        def a1_pe(pe):
            pe.wait_ge(S["f0_added"], NC * NE)
            for c in range(NC):
                pe.wait_ge(S["x1_ready"], c + 1)
                turn_pe(pe, TURN_F0 + c, c, lambda i: Y[:, c * TPC + i, :])
            pe.wait_ge(S["a1_lprod_ready"], 1)
            pe.matmul(ps_o[:, 0:2 * H1], ones[:, :], a1_lprod[:, :, :], start=True, stop=True)\
                .then_inc(S["a1_lsum_in"], 1)
            pe.wait_ge(S["x_lo"], TURN_F0 + NC)
            pe.wait_ge(S["a1_w_lo"], 1)
            for i, (kind, half) in enumerate(A1_FIRST):
                pe.wait_ge(S["a1_split_lo"], i)
                a1_pe_piece(pe, (kind, 0, half))
            pe.wait_ge(S["a1_lexped"], 1)

            def body(h, first, last):
                for s in range(SLOTS):
                    g = h * SLOTS + s
                    b, q = s // KT, s % KT
                    if s % KT == 0:
                        pe.wait_ge(S["a1_split_lo"], a1_splits(h, s - 1, last))
                    a1_pe_scores(pe, g, b, q, 0)
                    if not (first and s < 3):
                        pe.wait_ge(S["a1_split_lo"], a1_splits(h, s - 1, last))
                        a1_pe_turn_o(pe, g - 3, (s - 3) % 2)
                    if not (first and s < 2):
                        a1_pe_pv(pe, g - 2, ((s - 2) % SLOTS) // KT, 0)
                    if not (first and s < 3):
                        if s == 3 or s == KT + 3:
                            pe.wait_ge(S["a1_wo_scaled"], 2 * h + (1 + b))
                        a1_pe_out(pe, g - 3, (s - 3) % 2, ((s - 3) % SLOTS) // KT)
                    if not (first and s < 2):
                        a1_pe_pv(pe, g - 2, ((s - 2) % SLOTS) // KT, 1)
                    pieces = a1_pieces(s, last)
                    if s % KT == 0 and pieces:
                        pe.wait_ge(S["a1_w_lo"], 2 * h + (2 if s == 0 else 3))
                    if pieces:
                        pe.wait_ge(S["a1_added"], from0(g - 2))
                        pe.wait_ge(S["a1_split_lo"], a1_splits(h, s - 1, last))
                        a1_pe_piece(pe, pieces[0])
                    a1_pe_scores(pe, g, b, q, 1)
                    if len(pieces) > 1:
                        pe.wait_ge(S["a1_split_lo"], a1_splits(h, s, last, 1))
                        a1_pe_piece(pe, pieces[1])
                    if not (first and s < 1):
                        a1_pe_turn(pe, g - 1, (s - 1) % 2)

            heads(pe, H1, body)
            g = H1 * SLOTS
            a1_pe_turn_o(pe, g - 3, 1)
            a1_pe_pv(pe, g - 2, 1, 0)
            a1_pe_out(pe, g - 3, 1, 1)
            a1_pe_pv(pe, g - 2, 1, 1)
            a1_pe_turn(pe, g - 1, 1)
            a1_pe_turn_o(pe, g - 2, 0)
            a1_pe_pv(pe, g - 1, 1, 0)
            a1_pe_out(pe, g - 2, 0, 1)
            a1_pe_pv(pe, g - 1, 1, 1)
            a1_pe_turn_o(pe, g - 1, 1)
            a1_pe_out(pe, g - 1, 1, 1)

        def a1_act(act):
            for c in range(NC):
                turn_act(act, TURN_F0 + c, c)
            act.wait_ge(S["a1_lsum_in"], 1)
            act.activation(a1_lexp[:, :, :], ps_o[:, 0:2 * H1].rearrange("p (m h) -> p m h", m=2), ACT.Exp)\
                .then_inc(S["a1_lexped"], 1)
            for i, (kind, half) in enumerate(A1_FIRST):
                a1_act_piece(act, i + 1, (kind, 0, half))

            def at_hi(g):
                act.wait_ge(S["a1_pv"], g)
                for half in range(2):
                    act.wait_ge(S["a1_turned"], 2 * g + (half + 1))
                    act.activation(a1_ath[:, half * 4:half * 4 + 4, :],
                                   ps_t[:, half, :].rearrange("p (t c) -> p t c", c=P), ACT.Copy)\
                        .then_inc(S["a1_pt_hi"], 1)

            def ot_out(g, par):
                act.wait_ge(S["a1_ot_in"], g + 1)
                act.activation(a1_ot[par][:, :], ps_m[:, 0:2 * P], ACT.Copy).then_inc(S["a1_ot_out"], 1)

            def softmax(g, par, m):
                act.wait_ge(S["a1_negmaxed"], 2 * g + (m + 1))
                act.activation(a1_p[par][m][:, :], ps_s[:, m, :, :], ACT.Exp, bias=a1_negmax[:, par, m:m + 1],
                               accum_out=a1_sum[:, par, m:m + 1]).then_inc(S["a1_exped"], 1)

            def sum_square(g, par):
                act.wait_ge(S["a1_pv"], g + 1)
                act.activation(a1_sq[:, :], ps_o[:, 0:DV1], ACT.Square, scale=a1_rsum[:, par, 0:1],
                               accum_out=a1_ss[:, par:par + 1]).then_inc(S["a1_squared"], 1)

            def body(h, first, last):
                for s in range(SLOTS):
                    g = h * SLOTS + s
                    if not (first and s < 2):
                        at_hi(g - 2)
                    if not (first and s < 1):
                        softmax(g - 1, (s - 1) % 2, 1)
                    if not (first and s < 3):
                        ot_out(g - 3, (s - 3) % 2)
                    softmax(g, s % 2, 0)
                    if not (first and s < 2):
                        sum_square(g - 2, s % 2)
                    for i, piece in enumerate(a1_pieces(s, last)):
                        a1_act_piece(act, a1_splits(h, s, last, i + 1), piece)

            heads(act, H1, body)
            g = H1 * SLOTS
            at_hi(g - 2)
            softmax(g - 1, 1, 1)
            ot_out(g - 3, 1)
            sum_square(g - 2, 0)
            at_hi(g - 1)
            ot_out(g - 2, 0)
            sum_square(g - 1, 1)
            ot_out(g - 1, 1)

        def a1_dve(dve):
            for c in range(NC):
                turn_dve(dve, TURN_F0 + c, c, ps_t[:, c % 2, :])
            dve.wait_ge(S["x_turned"], TURN_F0 + NC)
            dve.memset(Y[:, :, :], 0.0)
            def step(ins):
                ins.then_inc(S["dve_step"], 1)
                dve.wait_ge(S["dve_step"], dve_steps.next())

            dve.wait_ge(S["a1_lam_loaded"], 16)
            lam = a1_lam[:, :, :].rearrange("p (m w) h -> p m w h", w=2)
            dve.tensor_tensor(a1_lprod[:, :, :], lam[:, :, 0, :], lam[:, :, 1, :], ALU.mult)\
                .then_inc(S["a1_lprod_ready"], 1)
            dve.wait_ge(S["a1_lexped"], 1)
            step(dve.tensor_tensor(a1_neglam[:, :], a1_lexp[:, 1, :], a1_lexp[:, 0, :], ALU.subtract))
            step(dve.tensor_scalar(a1_neglam[:, :], a1_neglam[:, :], -LAMBDA_INIT, None, ALU.add))
            for i, (kind, half) in enumerate(A1_FIRST):
                a1_dve_piece(dve, i + 1, (kind, 0, half))

            def negmax(g, par, m):
                dve.wait_ge(S["a1_scores"], 2 * g + (m + 1))
                dve.tensor_reduce(a1_negmax[:, par, m:m + 1], ps_s[:, m, :, :], AX.XY, ALU.max, negate=True)\
                    .then_inc(S["a1_negmaxed"], 1)

            def at_lo(g):
                for half in range(2):
                    dve.wait_ge(S["a1_pt_hi"], 2 * g + (half + 1))
                    tiles = slice(half * 4, half * 4 + 4)
                    dve.tensor_tensor(a1_atl[:, tiles, :], ps_t[:, half, :].rearrange("p (t c) -> p t c", c=P),
                                      a1_ath[:, tiles, :], ALU.subtract).then_inc(S["a1_pt_lo"], 1)

            def add_out(g, tok_tile):
                dve.wait_ge(S["a1_out_in"], g + 1)
                y = Y[:, tok_tile, :]
                dve.tensor_tensor(y, ps_m[:, 2 * P:3 * P], y, ALU.add).then_inc(S["a1_added"], 1)

            def factors(g, h, par):
                dve.wait_ge(S["a1_exped"], 2 * g + 2)
                dve.wait_ge(S["a1_combined"], from0(g - 1))
                dve.wait_ge(S["a1_o_normed"], from0(g - 1))
                dve.reciprocal(a1_rsum[:, par, :], a1_sum[:, par, :]).then_inc(S["a1_rsummed"], 1)
                dve.wait_ge(S["a1_rsummed"], g + 1)
                dve.sem_inc(S["waited"], 1)
                dve.scalar_tensor_tensor(out=a1_c[:, par:par + 1], in0=a1_rsum[:, par, 1:2],
                                         scalar=a1_sum[:, par, 0:1], in1=a1_neglam[:, bass.ds(h, 1)],
                                         op0=ALU.mult, op1=ALU.mult).then_inc(S["a1_c_ready"], 1)

            def combine(g, par):
                dve.wait_ge(S["a1_c_ready"], g + 1)
                p1, p2 = (a1_p[par][m][:, :] for m in range(2))
                dve.scalar_tensor_tensor(out=p1, in0=p2, scalar=a1_c[:, par:par + 1], in1=p1,
                                         op0=ALU.mult, op1=ALU.add).then_inc(S["a1_combined"], 1)

            def norm_o(g, par):
                dve.wait_ge(S["a1_rms_ready"], g + 1)
                dve.wait_ge(S["a1_ot_in"], from0(g - 1))
                dve.tensor_scalar(a1_on[par][:, :], ps_o[:, 0:DV1], a1_r[:, par:par + 1], a1_rsum[:, par, 0:1],
                                  ALU.mult, ALU.mult).then_inc(S["a1_o_normed"], 1)

            def body(h, first, last):
                for s in range(SLOTS):
                    g = h * SLOTS + s
                    if not (first and s < 2):
                        at_lo(g - 2)
                    negmax(g, s % 2, 0)
                    if not (first and s < 1):
                        factors(g - 1, h if s else h - 1, (s - 1) % 2)
                    if not (first and s < 3):
                        add_out(g - 3, (s - 3) % SLOTS)
                    if not (first and s < 1):
                        combine(g - 1, (s - 1) % 2)
                    pieces = a1_pieces(s, last)
                    if pieces:
                        a1_dve_piece(dve, a1_splits(h, s, last, 1), pieces[0])
                    negmax(g, s % 2, 1)
                    if not (first and s < 2):
                        norm_o(g - 2, s % 2)
                    if len(pieces) > 1:
                        a1_dve_piece(dve, a1_splits(h, s, last, 2), pieces[1])

            heads(dve, H1, body)
            g = H1 * SLOTS
            at_lo(g - 2)
            factors(g - 1, H1 - 1, 1)
            combine(g - 1, 1)
            add_out(g - 3, SLOTS - 3)
            norm_o(g - 2, 0)
            at_lo(g - 1)
            add_out(g - 2, SLOTS - 2)
            norm_o(g - 1, 1)
            add_out(g - 1, SLOTS - 1)

        def a1_pool(pool):
            def weights(count, h, b):
                pool.wait_ge(S["a1_w_loaded"][b], h * 16 + 16)
                pool.sem_inc(S["waited"], 1)
                pool.tensor_scalar(a1_w_hi[b][:, :], a1_w_raw[b][:, :], 1.0, 0.0, ALU.mult, ALU.add)\
                    .then_inc(S["a1_w_hi"], 1)
                pool.wait_ge(S["a1_w_hi"], count)
                pool.tensor_tensor(a1_w_lo[b][:, :], a1_w_raw[b][:, :], a1_w_hi[b][:, :], ALU.subtract)\
                    .then_inc(S["a1_w_lo"], 1)

            def out_weights(h, b):
                if b == 0:
                    pool.wait_ge(S["a1_wo_loaded"], h * 16 + 16)
                    pool.sem_inc(S["waited"], 1)
                for j in range(2):
                    ins = pool.tensor_scalar(a1_wo[b][:, j, :], a1_wo_raw[:, j, :], a1_rms[:, j:j + 1],
                                             1.0 - LAMBDA_INIT, ALU.mult, ALU.mult)
                ins.then_inc(S["a1_wo_scaled"], 1)

            weights(1, 0, 0)
            weights(2, 0, 1)
            pool.wait_ge(S["a1_rms_loaded"], 16)
            out_weights(0, 0)

            def rms(g, par):
                pool.wait_ge(S["a1_squared"], g + 1)
                pool.sem_inc(S["waited"], 1)
                r = a1_r[:, par:par + 1]
                pool.tensor_scalar(r, a1_ss[:, par:par + 1], 1.0 / DV1, EPS_RMS1, ALU.mult, ALU.add).then_inc(S["a1_rms_eps"], 1)
                pool.wait_ge(S["a1_rms_eps"], g + 1)
                pool.tensor_tensor(r, r, minus_half[:, 0:1], ALU.pow).then_inc(S["a1_rms_ready"], 1)

            def body(h, first, last):
                for s in range(SLOTS):
                    g = h * SLOTS + s
                    if not (first and s < 2):
                        rms(g - 2, s % 2)
                    if s == 1 and not last:
                        pool.wait_ge(S["a1_split_in"], a1_splits(h, -1, last))
                        weights(2 * h + 3, h + 1, 0)
                    if s == 3:
                        pool.wait_ge(S["a1_out_in"], h * SLOTS)
                        pool.sem_inc(S["waited"], 1)
                        out_weights(h, 1)
                    if s == KT + 1 and not last:
                        pool.wait_ge(S["a1_split_in"], a1_splits(h, KT - 1, last))
                        weights(2 * h + 4, h + 1, 1)
                    if s == KT + 3 and not last:
                        pool.wait_ge(S["a1_out_in"], h * SLOTS + KT)
                        pool.sem_inc(S["waited"], 1)
                        out_weights(h + 1, 0)

            heads(pool, H1, body)
            rms(H1 * SLOTS - 2, 0)
            rms(H1 * SLOTS - 1, 1)

        def a1_sp(sp):
            sp.wait_ge(S["x1_ready"], NC)
            for b in range(B):
                sp.dma_start(a1_w_raw[b][:, :], t["l1_w"][0]).then_inc(S["a1_w_loaded"][b], 16)
            sp.dma_start(a1_lam[:, :, :], t["l1_lam"]).then_inc(S["a1_lam_loaded"], 16)
            sp.dma_start(a1_rms[:, :], t["l1_rms"]).then_inc(S["a1_rms_loaded"], 16)
            wo_raw = a1_wo_raw[:, :, :].rearrange("p a b -> p (a b)")
            sp.dma_start(wo_raw, t["l1_wo"][0]).then_inc(S["a1_wo_loaded"], 16)

            def body(h, first, last):
                if last:
                    return
                for b in range(B):
                    sp.wait_ge(S["a1_w_lo"], 2 * h + (b + 1))
                    sp.dma_start(a1_w_raw[b][:, :], row(t["l1_w"], h + 1)).then_inc(S["a1_w_loaded"][b], 16)
                sp.wait_ge(S["a1_wo_scaled"], 2 * h + 2)
                sp.dma_start(wo_raw, row(t["l1_wo"], h + 1)).then_inc(S["a1_wo_loaded"], 16)

            heads(sp, H1, body)

        F1_ITEMS = 3 * HT

        def f1_pre_dve(dve):
            for c in range(NC):
                dve.wait_ge(S["x_turned"], from0(TURN_A1 + c - 1))
                y_tile = lambda i: tile(Y, c * TPC + i)
                if c == 0:
                    dve.wait_ge(S["a1_added"], H1 * SLOTS)
                add_and_norm(dve, NORM_A1 + 2 * c, c, y_tile, lambda i: tile(xst[c % 2], i))\
                    .then_inc(S["xst_ready"], 1)
                turn_dve(dve, TURN_A1 + c, c, ps_t[:, c % 2, :])
            for w0 in range(0, f1_w.shape[1], BANK):
                ws = slice(w0, min(w0 + BANK, f1_w.shape[1]))
                if w0 == 0:
                    dve.wait_ge(S["f1_loaded"], 32)
                ins = dve.tensor_copy(f1_w[:, ws], f1_raw[:, ws])
            ins.then_inc(S["f1_w_ready"], 1)

        def f1_pre_pool(pool):
            for c in range(NC):
                norm_rstd(pool, NORM_A1 + 2 * c, 0)
                norm_rstd(pool, NORM_A1 + 2 * c + 1, 1)

        def f1_pre_pe(pe):
            for c in range(NC):
                pe.wait_ge(S["xst_ready"], 2 * NC + c + 1)
                turn_pe(pe, TURN_A1 + c, c, lambda i: xst[c % 2][:, i, :])

        def f1_pre_act(act):
            for c in range(NC):
                turn_act(act, TURN_A1 + c, c)

        def f1_bank(use):
            return ps_s[:, use % 4 // 2, use % 2, :]

        def f1_pe(pe):
            pe.wait_ge(S["f1_w_ready"], 1)
            pe.wait_ge(S["x_lo"], 4 * NC)
            with pe.Fori(0, NC) as c:
                x = bass.ds(c * BANK, BANK)
                for ht in range(HT):
                    for w in range(2):
                        if ht < 2:
                            pe.wait_ge(S["f1_gelued"], c * (2 * HT))
                        else:
                            pe.wait_ge((S["f1_silued"], S["f1_gated"])[w], from0(c * HT + (ht - 1)))
                        cols = slice(ht * P, (ht + 1) * P)
                        pe.matmul(f1_bank(2 * ht + w), f1_w12[:, w, cols], xT_hi[:, x], start=True, stop=False)
                        pe.matmul(f1_bank(2 * ht + w), f1_w12[:, w, cols], xT_lo[:, x], start=False, stop=True)\
                            .then_inc(S["f1_pre"], 1)
                for layer in range(2):
                    for ot in range(HT):
                        if layer == 0:
                            pe.wait_ge((S["f1_silued"], S["f1_gated"])[ot % 2], c * HT + (3 + ot // 2))
                        else:
                            pe.wait_ge(S["f1_gelued"], c * (2 * HT) + (ot + 1))
                        cols = slice(ot * P, (ot + 1) * P)
                        for kt in range(HT):
                            if ot == 0:
                                pe.wait_ge(S["f1_split"], c * F1_ITEMS + (HT * layer + kt + 1))
                            w = f1_wh[:, layer, kt, cols]
                            pe.matmul(f1_bank(ot), w, f1_hi[layer][kt][:, :], start=kt == 0, stop=False)
                            ins = pe.matmul(f1_bank(ot), w, f1_lo[layer][kt][:, :], start=False, stop=kt == HT - 1)
                        ins.then_inc(S["f1_hidden"], 1)
                pe.wait_ge(S["f1_y_out"], c)
                for kt in range(HT):
                    pe.wait_ge(S["f1_split"], c * F1_ITEMS + (2 * HT + kt + 1))
                    pe.matmul(ps_o[:, :], f1_w3[:, kt, :], f1_hi[0][kt][:, :], start=kt == 0, stop=False)
                    ins = pe.matmul(ps_o[:, :], f1_w3[:, kt, :], f1_lo[0][kt][:, :], start=False, stop=kt == HT - 1)
                ins.then_inc(S["f1_down"], 1)
                pe.wait_ge(S["f1_y_out"], c + 1)
                pe.wait_ge(S["f1_y_used"], c)
                for i in range(TPC):
                    ins = pe.transpose(ps_t[:, 0, i * P:(i + 1) * P], f1_y[0][:, i * P:(i + 1) * P], ident[:, :])
                ins.then_inc(S["f1_y_turned"], 1)

        def f1_act(act):
            act.wait_ge(S["f1_s_loaded"], 16)
            with act.Fori(0, NC) as c:
                for ht in range(HT):
                    act.wait_ge(S["f1_pre"], c * (2 * HT) + (2 * ht + 1))
                    act.wait_ge(S["f1_gated"], from0(c * HT + max(ht - 1, 0)))
                    act.activation(f1_a[ht % 2][:, :], f1_bank(2 * ht), ACT.Silu, scale=f1_s[:, ht:ht + 1])\
                        .then_inc(S["f1_silued"], 1)
                for layer in range(2):
                    for ot in range(HT):
                        item = HT * (layer + 1) + ot
                        k = item + HT
                        act.wait_ge(S["f1_hidden"], c * (2 * HT) + (HT * layer + ot + 1))
                        act.wait_ge(S["f1_split"], from0(c * F1_ITEMS + (item - 1)))
                        act.activation(f1_f[item % 2][:, :], f1_bank(ot), ACT.Gelu, scale=f1_s[:, k:k + 1])\
                            .then_inc(S["f1_gelued"], 1)
                act.wait_ge(S["f1_down"], c + 1)
                act.wait_ge(S["f1_y_turned"], c)
                act.activation(f1_y[0][:, :], ps_o[:, :], ACT.Copy, scale=f1_s[:, 4 * HT:4 * HT + 1])\
                    .then_inc(S["f1_y_out"], 1)

        def f1_dve(dve):
            with dve.Fori(0, NC) as c:
                dve_steps.enter(c, 2)
                for item in range(F1_ITEMS):
                    f = f1_f[item % 2][:, :]
                    if item < HT:
                        dve.wait_ge(S["f1_silued"], c * HT + (item + 1))
                        dve.wait_ge(S["f1_pre"], c * (2 * HT) + (2 * item + 2))
                        dve.scalar_tensor_tensor(out=f, in0=f1_bank(2 * item + 1), scalar=f1_s[:, HT + item:HT + item + 1],
                                                 in1=f1_a[item % 2][:, :], op0=ALU.mult, op1=ALU.mult)\
                            .then_inc(S["f1_gated"], 1)
                        dve.wait_ge(S["f1_gated"], c * HT + (item + 1))
                    else:
                        dve.wait_ge(S["f1_gelued"], c * (2 * HT) + (item - HT + 1))
                    layer, kt = item // HT % 2, item % HT
                    dve.tensor_copy(f1_hi[layer][kt][:, :], f).then_inc(S["f1_hi_ready"], 1)
                    dve.wait_ge(S["f1_hi_ready"], c * F1_ITEMS + (item + 1))
                    dve.tensor_tensor(f1_lo[layer][kt][:, :], f, f1_hi[layer][kt][:, :], ALU.subtract)\
                        .then_inc(S["f1_split"], 1)
                dve.wait_ge(S["f1_y_turned"], c + 1)
                dve.sem_inc(S["waited"], 1)
                n = c + NORM_F1
                src = lambda i: bank_tile(ps_t[:, 0, :], i)
                norm_stats(dve, n, 0, src)
                ins = norm_apply(dve, n, 0, src, lambda i: tile(xhat, i))
                ins.then_inc(S["f1_y_used"], 1)
                dve.wait_ge(S["f1_y_used"], c + 1)
                xc = X[:, bass.ds(c * TPC, TPC), :]
                dve.tensor_tensor(xc, xc, xhat[:, :, :], ALU.add).then_inc(S["dve_step"], 1)
                dve.wait_ge(S["dve_step"], dve_steps.next())
                dve.sem_inc(S["waited"], 1)
                dve_steps.leave(NC)

        def f1_pool(pool):
            with pool.Fori(0, NC) as c:
                pool_steps.enter(c, 1)
                norm_rstd(pool, c + NORM_F1, 0)
                pool_steps.leave(NC)

        def f1_load_sp(sp):
            sp.wait_ge(S["a1_added"], H1 * SLOTS)
            half = f1_raw.shape[1] // 2
            sp.dma_start(f1_raw[:, 0:half], t["ffn1_w"][:, 0:half]).then_inc(S["f1_loaded"], 16)
            sp.dma_start(f1_raw[:, half:], t["ffn1_w"][:, half:]).then_inc(S["f1_loaded"], 16)
            sp.dma_start(f1_s[:, :], t["ffn1_s"]).then_inc(S["f1_s_loaded"], 16)

        def f1_sp(sp):
            base = steps_before_f1[0]
            for c in range(NC):
                sp.wait_ge(S["dve_step"], base + 2 * (c + 1))
                sp.dma_start(out_dram[:, c * TPC:(c + 1) * TPC, :], X[:, c * TPC:(c + 1) * TPC, :])\
                    .then_inc(S["out_stored"], 16)
            sp.wait_ge(S["out_stored"], 16 * NC)

        steps_before_f1 = []
        block = ctx.enter_context(nc.Block())

        @block.vector
        def _(dve):
            input_dve(dve)
            a0_dve(dve)
            f0_pre_dve(dve)
            f0_dve(dve)
            a1_dve(dve)
            f1_pre_dve(dve)
            steps_before_f1.append(dve_steps.base + dve_steps.n)
            f1_dve(dve)

        @block.tensor
        def _(pe):
            input_pe(pe)
            a0_pe(pe)
            f0_pre_pe(pe)
            f0_pe(pe)
            a1_pe(pe)
            f1_pre_pe(pe)
            f1_pe(pe)

        @block.scalar
        def _(act):
            input_act(act)
            a0_act(act)
            f0_pre_act(act)
            f0_act(act)
            a1_act(act)
            f1_pre_act(act)
            f1_act(act)

        @block.gpsimd
        def _(pool):
            input_pool(pool)
            a0_pool(pool)
            f0_pre_pool(pool)
            f0_pool(pool)
            a1_pool(pool)
            f1_pre_pool(pool)
            f1_pool(pool)

        @block.sync
        def _(sp):
            input_sp(sp)
            a0_sp(sp)
            f0_sp(sp)
            a1_sp(sp)
            f1_load_sp(sp)
            f1_sp(sp)


def kernel(**inputs):
    import numpy as np
    import concourse.bacc as bacc
    from concourse import mybir as mb
    from concourse.bass_utils import run_bass_kernel_spmd

    w = {k: np.asarray(v) for k, v in inputs.items()}
    D, H0, DH0, H1, HID, E = 128, 16, 64, 8, 512, 8
    qkv = w["L0_attn_W_qkv"].reshape(D, H0, DH0, 3).transpose(3, 1, 0, 2)
    wo0 = w["L0_attn_W_out"].reshape(H0, DH0, D)
    w1 = np.concatenate([w["L0_ffn_ew1"], w["L0_ffn_sw1"][None]])
    w2 = np.concatenate([w["L0_ffn_ew2"], w["L0_ffn_sw2"][None]])
    b1 = np.concatenate([w["L0_ffn_eb1"], w["L0_ffn_sb1"][None]])
    b2 = np.concatenate([w["L0_ffn_eb2"], w["L0_ffn_sb2"][None]])
    by_head = lambda a: a.reshape(H1, 2 * D, D).transpose(0, 2, 1)
    q, k, v = (by_head(w[f"L1_attn_W{n}"]) for n in "qkv")
    lam = np.stack([w[f"L1_attn_lambda_{n}"].T for n in ("q1", "k1", "q2", "k2")], axis=1)
    tiled = lambda a: a.T.reshape(-1, D, a.shape[0]).transpose(1, 0, 2).reshape(D, -1)
    col = lambda a: a.reshape(-1, D).T
    arrays = {
        "x": w["L0_attn_X"],
        "l0_wqk": np.concatenate([qkv[0], qkv[0], qkv[1], qkv[1]], axis=2),
        "l0_wv": np.concatenate([qkv[2], qkv[2]], axis=2),
        "l0_wo": np.concatenate([wo0, wo0], axis=1),
        "ffn0_w1": w1.transpose(1, 0, 2),
        "ffn0_w2": w2.reshape(E + 1, HID // D, D, D).transpose(2, 0, 1, 3),
        "ffn0_b1": b1.reshape(E + 1, HID // D, D).transpose(2, 0, 1),
        "ffn0_b2": b2,
        "ffn0_nw": w["L0_ffn_norm_weight"].reshape(D, 1),
        "ffn0_rw": w["L0_ffn_router_w"].T,
        "l1_w": np.concatenate([q, k, v], axis=2),
        "l1_wo": w["L1_attn_Wo"].reshape(D, H1, 2, D).transpose(1, 3, 2, 0).reshape(H1, D, 2 * D),
        "l1_lam": lam,
        "l1_rms": col(w["L1_attn_rms_scale"]),
        "ffn1_w": np.concatenate([tiled(w[f"L1_ffn_{n}_w"]) for n in ("w1", "w2", "h1", "h2", "w3")], axis=1),
        "ffn1_s": np.concatenate([col(w[f"L1_ffn_{n}_s"]) for n in ("w1", "w2", "h1", "h2", "w3")], axis=1),
    }
    arrays = {k: np.ascontiguousarray(a) for k, a in arrays.items()}
    nc = bacc.Bacc("TRN2", target_bir_lowering=False, num_devices=1)
    aps = {k: nc.dram_tensor(f"in_{k}", a.shape, mb.dt.from_np(a.dtype), kind="ExternalInput").ap()
           for k, a in arrays.items()}
    out = nc.dram_tensor("out", w["L0_attn_X"].shape, mb.dt.from_np(np.dtype("float32")), kind="ExternalOutput").ap()
    sandwich_kernel(nc, aps, out)
    r = run_bass_kernel_spmd(nc, [{f"in_{k}": a for k, a in arrays.items()}], core_ids=[0])
    return r.results[0]["out"]
```

```python
import math
from contextlib import ExitStack

import concourse.bass as bass
from concourse import mybir

F32 = mybir.dt.float32
F32R = mybir.dt.float32r
ALU = mybir.AluOpType
ACT = mybir.ActivationFunctionType
AX = mybir.AxisListType

P = 128
EPS_LN = 1e-5
EPS_RMS0 = 1e-8
EPS_TOPK = 1e-6
EPS_RMS1 = 1e-5
LAMBDA_INIT = 0.8 - 0.6 * math.exp(-0.3 * 1)
BANK = 512


def sandwich_kernel(nc, t, out):
    B, SEQ, D = t["x"].shape
    TOK = B * SEQ
    NT = TOK // P
    NC = TOK // BANK
    TPC = BANK // P
    KT = SEQ // P
    H0, DH0 = t["l0_wv"].shape[0], 64
    H1, DH1 = t["l1_w"].shape[0], 128
    DV1 = 2 * DH1
    NE = t["ffn0_w1"].shape[1]
    NR = NE - 1
    HID = t["ffn0_w1"].shape[2]
    HT = HID // P
    SLOTS = B * KT
    assert D == P and B == 2 and KT == 8 and SEQ == 2 * BANK and HT == 4

    ctx = ExitStack()
    with ctx:
        def sem(name):
            return ctx.enter_context(nc.semaphore(name))

        def sb_in(scope):
            used = [0]

            def buffer(name, shape, dt=F32):
                if name is None:
                    assert used[0] <= shape, used
                    name, shape = f"pad{len(pads)}", [P, (shape - used[0]) // 4]
                    pads.append(name)
                    if shape[1] == 0:
                        return None
                size = 4
                for n in shape[1:]:
                    size *= n
                used[0] += size
                return scope.enter_context(nc.sbuf_tensor(name, shape, dt))
            return buffer

        pads = []
        KB = 1024
        LOW = 94 * KB
        A0_END = 129 * KB

        ps_s = ctx.enter_context(nc.psum_tensor("ps_s", [P, 2, 2, BANK], F32))
        ps_t = ctx.enter_context(nc.psum_tensor("ps_t", [P, 2, BANK], F32))
        ps_o = ctx.enter_context(nc.psum_tensor("ps_o", [P, BANK], F32))
        ps_m = ctx.enter_context(nc.psum_tensor("ps_m", [P, BANK], F32))

        sb = sb_in(ctx)
        X = sb("X", [P, NT, D])
        ident = sb("ident", [P, P])
        xT_hi = sb("xT_hi", [P, TOK], F32R)
        xT_lo = sb("xT_lo", [P, TOK], F32R)
        stats = sb("stats", [P, 4, TPC, 6])
        mv = sb("mv", [P, 4, TPC, 2])
        rstd = sb("rstd", [P, 4, TPC])
        xhat = sb("xhat", [P, TPC, D])
        xst = [sb(f"xst{i}", [P, TPC, D]) for i in range(2)]
        ones = sb("ones", [P, P])
        minus_half = sb("minus_half", [P, TPC])
        Y = sb("Y", [P, NT, D])
        Yflat = Y[:, :, :].rearrange("p t d -> p (t d)")

        scope = ExitStack()
        sb = sb_in(scope)
        xT_f = sb("xT_f", [P, TOK])
        a0_wqk_raw = sb("a0_wqk_raw", [P, 2 * DH0])
        a0_wqk_hi = sb("a0_wqk_hi", [P, 2 * DH0], F32R)
        a0_wqk_lo = sb("a0_wqk_lo", [P, 2 * DH0], F32R)
        a0_wv = sb("a0_wv", [P, 2 * DH0])
        a0_wo = sb("a0_wo", [P, D])
        a0_q = [sb(f"a0_q{b}", [P, SEQ], F32R) for b in range(B)]
        a0_kh = [sb(f"a0_kh{b}", [P, SEQ], F32R) for b in range(B)]
        a0_kl = [sb(f"a0_kl{b}", [P, SEQ], F32R) for b in range(B)]
        a0_v = [sb(f"a0_v{b}", [P, KT, 2 * DH0], F32R) for b in range(B)]
        a0_p = [sb(f"a0_p{i}", [P, SEQ]) for i in range(4)]
        a0_pth = [sb(f"a0_pth{i}", [P, KT, BANK], F32R) for i in range(2)]
        a0_ptl = [sb(f"a0_ptl{i}", [P, KT, BANK], F32R) for i in range(2)]
        a0_o = [sb(f"a0_o{i}", [P, BANK]) for i in range(2)]
        a0_negmax = sb("a0_negmax", [P, 4])
        a0_sum = sb("a0_sum", [P, 4])
        a0_rsum = sb("a0_rsum", [P, 4])
        sb(None, A0_END)
        scope.close()

        scope = ExitStack()
        sb = sb_in(scope)
        f0_w1_hi = sb("f0_w1_hi", [P, NE, HID], F32R)
        f0_w1_lo = sb("f0_w1_lo", [P, NE, HID], F32R)
        f0_w2 = sb("f0_w2", [P, NE, HT, D])
        f0_b1 = sb("f0_b1", [P, NE, HT])
        f0_b2 = sb("f0_b2", [NE, D])
        f0_nw = sb("f0_nw", [P, 1])
        f0_rw = sb("f0_rw", [P, NR])
        f0_nT = [sb(f"f0_nT{i}", [P, BANK]) for i in range(2)]
        f0_h = [[sb(f"f0_h{i}{j}", [P, BANK]) for j in range(HT)] for i in range(2)]
        f0_rank = sb("f0_rank", [P, NR])
        f0_prob = sb("f0_prob", [P, NT, NR])
        f0_left = sb("f0_left", [P, NT, NR])
        f0_tmp = sb("f0_tmp", [P, NT, NR])
        f0_tmp2 = sb("f0_tmp2", [P, NT, NR])
        f0_one = [sb(f"f0_one{i}", [P, NT, NR]) for i in range(2)]
        f0_top = [sb(f"f0_top{i}", [P, NT]) for i in range(2)]
        f0_idx = sb("f0_idx", [P, NT])
        f0_den = sb("f0_den", [P, NT])
        f0_comb = sb("f0_comb", [P, NT, NE])
        f0_combT = sb("f0_combT", [NE, TOK])
        sb(None, LOW)
        sb(None, A0_END)
        f0_w1_raw = sb("f0_w1_raw", [P, NE, HID])
        scope.close()

        scope = ExitStack()
        sb = sb_in(scope)
        WC = 4 * DH1 + DV1
        a1_hi = [[], [sb(f"a1_hi1{j}", [P, SEQ], F32R) for j in range(4)]]
        a1_lo = [[], [sb(f"a1_lo1{j}", [P, SEQ], F32R) for j in range(4)]]
        a1_vh = [sb(f"a1_vh{b}", [P, KT, DV1], F32R) for b in range(B)]
        a1_vl = [None, sb("a1_vl1", [P, KT, DV1], F32R)]
        a1_p = [[sb(f"a1_p{i}{m}", [P, SEQ]) for m in range(2)] for i in range(2)]
        a1_ath = sb("a1_ath", [P, KT, P], F32R)
        a1_sq = sb("a1_sq", [P, DV1])
        sb(None, LOW)
        a1_w_raw = [sb(f"a1_w_raw{b}", [P, WC]) for b in range(B)]
        a1_w_hi = [sb(f"a1_w_hi{b}", [P, WC], F32R) for b in range(B)]
        a1_w_lo = [sb(f"a1_w_lo{b}", [P, WC], F32R) for b in range(B)]
        a1_hi[0] = [sb(f"a1_hi0{j}", [P, SEQ], F32R) for j in range(4)]
        a1_lo[0] = [sb(f"a1_lo0{j}", [P, SEQ], F32R) for j in range(4)]
        a1_vl[0] = sb("a1_vl0", [P, KT, DV1], F32R)
        a1_atl = sb("a1_atl", [P, KT, P], F32R)
        a1_on = [sb(f"a1_on{i}", [P, DV1]) for i in range(2)]
        a1_ot = [sb(f"a1_ot{i}", [P, DV1]) for i in range(2)]
        a1_wo_raw = sb("a1_wo_raw", [P, 2, D])
        a1_wo = [sb(f"a1_wo{b}", [P, 2, D]) for b in range(B)]
        a1_rms = sb("a1_rms", [P, 2])
        a1_neglam = sb("a1_neglam", [P, H1])
        a1_lam = sb("a1_lam", [P, 4, H1])
        a1_lprod = sb("a1_lprod", [P, 2, H1])
        a1_lexp = sb("a1_lexp", [P, 2, H1])
        a1_negmax = sb("a1_negmax", [P, 2, 2])
        a1_sum = sb("a1_sum", [P, 2, 2])
        a1_rsum = sb("a1_rsum", [P, 2, 2])
        a1_c = sb("a1_c", [P, 2])
        a1_ss = sb("a1_ss", [P, 2])
        a1_r = sb("a1_r", [P, 2])
        scope.close()

        scope = ExitStack()
        sb = sb_in(scope)
        f1_a = [sb(f"f1_a{i}", [P, BANK]) for i in range(2)]
        f1_f = [sb(f"f1_f{i}", [P, BANK]) for i in range(4)]
        f1_hi = [[[sb(f"f1_hi{i}{k}{j}", [P, BANK], F32R) for j in range(HT)] for k in range(2)] for i in range(2)]
        f1_lo = [[[sb(f"f1_lo{i}{k}{j}", [P, BANK], F32R) for j in range(HT)] for k in range(2)] for i in range(2)]
        f1_y = [sb(f"f1_y{i}", [P, BANK]) for i in range(2)]
        sb(None, LOW)
        f1_raw = sb("f1_raw", [P, 2 * HID + 2 * HT * HID + HT * D])
        f1_w = sb("f1_w", [P, 2 * HID + 2 * HT * HID + HT * D], F32R)
        f1_s = sb("f1_s", [P, 4 * HT + 1])
        assert (2 * f1_w.shape[1] + f1_s.shape[1]) <= 6 * WC + 8 * SEQ
        scope.close()
        f1_w12 = f1_w[:, 0:2 * HID].rearrange("p (w n) -> p w n", w=2)
        f1_wh = f1_w[:, 2 * HID:2 * HID + 2 * HT * HID].rearrange("p (w k n) -> p w k n", w=2, k=HT)
        f1_w3 = f1_w[:, 2 * HID + 2 * HT * HID:].rearrange("p (k n) -> p k n", k=HT)

        x_dram = t["x"].rearrange("b (t p) d -> p (b t) d", p=P)
        out_dram = out.rearrange("b (t p) d -> p (b t) d", p=P)

        S = {name: ctx.enter_context(nc.semaphore(name)) for name in (
            "pool_step", "norm_var", "norm_rstd", "waited", "x_lo", "x_turned", "x_hi", "ident_ready", "xst_ready",
            "y_zero", "y0_turned", "x1_ready", "dve_step", "out_stored", "x_final",
            "a0_out_added", "a0_split_lo", "a0_split_in", "a0_o_out", "a0_out_in", "a0_p_normed", "a0_pt_lo",
            "a0_turned", "a0_pv", "a0_w_lo", "a0_wv_loaded", "a0_exped", "a0_scores", "a0_wo_loaded",
            "a0_split_hi", "a0_pt_hi", "a0_negmaxed", "a0_rsummed", "a0_wqk_loaded", "a0_w_hi",
            "a0_kh_copied", "a0_kl_copied",
            "f0_comb_ready", "f0_combT_in", "f0_combT_ready", "f0_small_loaded", "f0_bias_in", "f0_nT_ready",
            "f0_logits", "f0_exped", "f0_w1_hi_ready", "f0_y_started", "f0_w1_lo_ready", "f0_w2_loaded",
            "f0_relued", "f0_up", "f0_added", "f0_down",
            "a1_split_in", "a1_split_hi", "a1_split_lo", "a1_exped", "a1_scores", "a1_combined", "a1_pt_lo",
            "a1_turned", "a1_o_normed", "a1_pv", "a1_added", "a1_ot_in", "a1_ot_out", "a1_out_in",
            "a1_lprod_ready", "a1_lsum_in", "a1_w_lo", "a1_lexped", "a1_wo_scaled", "a1_pt_hi", "a1_negmaxed",
            "a1_squared", "a1_lam_loaded", "a1_rsummed", "a1_c_ready", "a1_rms_ready", "a1_w_hi",
            "a1_wo_loaded", "a1_rms_loaded", "a1_rms_eps", "a1_rms_power",
            "f1_loaded", "f1_w_ready", "f1_gelued", "f1_pre", "f1_split", "f1_hidden", "f1_y_out", "f1_down",
            "f1_y_used", "f1_y_turned", "f1_s_loaded", "f1_gated", "f1_silued", "f1_hi_ready",
        )}
        S["x_loaded"] = [ctx.enter_context(nc.semaphore(f"x_loaded{i}")) for i in range(NC)]
        S["f0_w1_loaded"] = [ctx.enter_context(nc.semaphore(f"f0_w1_loaded{i}")) for i in range(NE)]
        S["a1_w_loaded"] = [ctx.enter_context(nc.semaphore(f"a1_w_loaded{i}")) for i in range(B)]

        def from0(count):
            return max(count, 0) if isinstance(count, int) else count

        def row(ap, h):
            if isinstance(h, int):
                return ap[h]
            return ap[bass.ds(h, 1)].rearrange("a p n -> (a p) n")

        def heads(eng, count, body):
            body(0, True, False)
            with eng.Fori(1, count - 1) as h:
                body(h, False, False)
            body(count - 1, False, True)

        class Count:

            def __init__(self):
                self.base, self.n = 0, 0

            def next(self):
                self.n += 1
                return self.base + self.n

            def enter(self, i, per_round):
                self.start, self.per_round = self.base + self.n, per_round
                self.base, self.n = self.start + i * per_round, 0

            def leave(self, rounds):
                assert self.n == self.per_round, self.n
                self.base, self.n = self.start + rounds * self.per_round, 0

        dve_steps = Count()
        pool_steps = Count()

        NORM_IN = 0
        NORM_A0 = NORM_IN + NC
        NORM_F0 = NORM_A0 + 2 * NC
        NORM_A1 = NORM_F0 + 2 * NC
        NORM_F1 = NORM_A1 + 2 * NC

        def norm_stats(dve, n, par, src):
            for i in range(TPC):
                ins = dve.bn_stats(stats[:, par, i, :], src(i))
            ins.then_inc(S["dve_step"], 1)
            dve.wait_ge(S["dve_step"], dve_steps.next())
            dve.sem_inc(S["waited"], 1)
            for i in range(TPC):
                ins = dve.bn_aggr(mv[:, par, i, :], stats[:, par, i, :])
            ins.then_inc(S["norm_var"], 1)

        def norm_apply(dve, n, par, src, dst):
            dve.wait_ge(S["norm_rstd"], n + 1)
            for i in range(TPC):
                ins = dve.tensor_scalar(dst(i), src(i), mv[:, par, i, 0:1], rstd[:, par, i:i + 1],
                                        ALU.subtract, ALU.mult)
            return ins

        def pool_rsqrt(pool, dst, src, eps):
            pool.tensor_scalar(dst, src, eps, None, ALU.add).then_inc(S["pool_step"], 1)
            pool.wait_ge(S["pool_step"], pool_steps.next())
            pool.sem_inc(S["waited"], 1)
            return pool.tensor_tensor(dst, dst, minus_half[:, 0:dst.shape[-1]], ALU.pow)

        def norm_rstd(pool, n, par):
            pool.wait_ge(S["norm_var"], n + 1)
            pool.sem_inc(S["waited"], 1)
            pool_rsqrt(pool, rstd[:, par, :], mv[:, par, :, 1], EPS_LN).then_inc(S["norm_rstd"], 1)

        def norm_rstd_rms(pool, n, par):
            pool.wait_ge(S["norm_var"], n + 1)
            pool.sem_inc(S["waited"], 1)
            pool.tensor_scalar(rstd[:, par, :], mv[:, par, :, 1], 1 + EPS_RMS0, EPS_LN * EPS_RMS0, ALU.mult, ALU.add)\
                .then_inc(S["pool_step"], 1)
            pool.wait_ge(S["pool_step"], pool_steps.next())
            pool.sem_inc(S["waited"], 1)
            pool.tensor_tensor(rstd[:, par, :], rstd[:, par, :], minus_half[:, 0:TPC], ALU.pow)\
                .then_inc(S["norm_rstd"], 1)

        def add_and_norm(dve, n, c, src, dst):
            norm_stats(dve, n, 0, src)
            norm_apply(dve, n, 0, src, lambda i: tile(xhat, i)).then_inc(S["dve_step"], 1)
            dve.wait_ge(S["dve_step"], dve_steps.next())
            dve.sem_inc(S["waited"], 1)
            xc = X[:, bass.ds(c * TPC, TPC), :]
            dve.tensor_tensor(xc, xc, xhat[:, :, :], ALU.add).then_inc(S["dve_step"], 1)
            dve.wait_ge(S["dve_step"], dve_steps.next())
            dve.sem_inc(S["waited"], 1)
            x_tile = lambda i: X[:, bass.ds(c * TPC + i, 1), :]
            norm_stats(dve, n + 1, 1, x_tile)
            return norm_apply(dve, n + 1, 1, x_tile, dst)

        def norm_pair(dve, stage, n, c, src):
            for i in range(2):
                par = c + i
                x_tile = lambda k: tile(X, (c + i) * TPC + k)
                staged = lambda k: tile(xst[i], k)
                from_tile = lambda k: src(i, k)
                if stage == 0:
                    norm_stats(dve, n + i, par, from_tile)
                elif stage == 1:
                    norm_apply(dve, n + i, par, from_tile, staged).then_inc(S["dve_step"], 1)
                    dve_steps.next()
                elif stage == 2:
                    if i == 0:
                        dve.wait_ge(S["dve_step"], dve_steps.base + dve_steps.n)
                    xc = X[:, (c + i) * TPC:(c + i + 1) * TPC, :]
                    dve.tensor_tensor(xc, xc, xst[i][:, :, :], ALU.add).then_inc(S["dve_step"], 1)
                    dve_steps.next()
                elif stage == 3:
                    if i == 0:
                        dve.wait_ge(S["dve_step"], dve_steps.base + dve_steps.n)
                    norm_stats(dve, n + 2 + i, par, x_tile)
                else:
                    norm_apply(dve, n + 2 + i, par, x_tile, staged).then_inc(S["xst_ready"], 1)

        def tile(buf, i):
            return buf[:, bass.ds(i, 1), :]

        def bank_tile(bank, i):
            return bank[:, i * P:(i + 1) * P].rearrange("p (a n) -> p a n", a=1)

        TURN_IN, TURN_A0, TURN_F0, TURN_A1 = 0, NC, 2 * NC, 3 * NC

        def turn_pe(pe, k, c, src):
            pe.wait_ge(S["x_lo"], from0(k - 1))
            for i in range(TPC):
                ins = pe.transpose(ps_t[:, c % 2, i * P:(i + 1) * P], src(i), ident[:, :])
            ins.then_inc(S["x_turned"], 1)

        def turn_act(act, k, c, scale=1.0):
            act.wait_ge(S["x_turned"], k + 1)
            act.activation(xT_hi[:, c * BANK:(c + 1) * BANK], ps_t[:, c % 2, :], ACT.Copy, scale=scale)\
                .then_inc(S["x_hi"], 1)

        def turn_dve(dve, k, c, src):
            dve.wait_ge(S["x_hi"], k + 1)
            cols = slice(c * BANK, (c + 1) * BANK)
            dve.tensor_tensor(xT_lo[:, cols], src, xT_hi[:, cols], ALU.subtract).then_inc(S["x_lo"], 1)

        def input_pe(pe):
            pe.wait_ge(S["ident_ready"], 2)
            for c in range(NC):
                pe.wait_ge(S["xst_ready"], c + 1)
                turn_pe(pe, TURN_IN + c, c, lambda i: xst[c % 2][:, i, :])

        def input_act(act):
            for c in range(NC):
                act.wait_ge(S["x_turned"], c + 1)
                act.activation(xT_f[:, c * BANK:(c + 1) * BANK], ps_t[:, c % 2, :], ACT.Copy)
                turn_act(act, TURN_IN + c, c)

        def input_dve(dve):
            dve.memset(ones[:, :], 1.0)
            dve.memset(Y[:, :, :], 0.0).then_inc(S["y_zero"], 1)

            def x_stats(c):
                dve.wait_ge(S["x_loaded"][c], 16)
                norm_stats(dve, NORM_IN + c, c, lambda i: tile(X, c * TPC + i))

            x_stats(0)
            x_stats(1)
            for c in range(NC):
                dve.wait_ge(S["x_turned"], from0(c - 1))
                norm_apply(dve, NORM_IN + c, c, lambda i: tile(X, c * TPC + i), lambda i: tile(xst[c % 2], i))\
                    .then_inc(S["xst_ready"], 1)
                if c < 2:
                    x_stats(c + 2)
                else:
                    turn_dve(dve, TURN_IN + c - 2, c - 2, ps_t[:, c % 2, :])
            for c in range(2, NC):
                turn_dve(dve, TURN_IN + c, c, ps_t[:, c % 2, :])

        def input_pool(pool):
            pool.memset(minus_half[:, :], -0.5).then_inc(S["pool_step"], 1)
            pool.wait_ge(S["pool_step"], pool_steps.next())
            pool.sem_inc(S["waited"], 1)
            pool.memset(ident[:, :], 0.0).then_inc(S["ident_ready"], 1)
            pool.wait_ge(S["ident_ready"], 1)
            pool.affine_select(out=ident[:, :], in_=ident[:, :], compare_op=ALU.not_equal, fill=1.0, base=0,
                               pattern=[[-1, P]], channel_multiplier=1).then_inc(S["ident_ready"], 1)
            for c in range(NC):
                norm_rstd(pool, NORM_IN + c, c)

        def input_sp(sp):
            for c in range(NC):
                sp.dma_start(X[:, c * TPC:(c + 1) * TPC, :], x_dram[:, c * TPC:(c + 1) * TPC, :])\
                    .then_inc(S["x_loaded"][c], 16)
                if c == 0:
                    a0_load_first(sp)

        A0_PIECES = {
            0: ("qk", 1, 0), 2: ("v", 0, 0), 3: ("out", -2), 4: ("qk", 1, 1), 5: ("v", 0, 1), 7: ("out", -1),
            8: ("v", 1, 0), 10: ("qk", 0, 0), 11: ("out", 0), 12: ("qk", 0, 1), 13: ("v", 1, 1), 15: ("out", 1)}
        A0_NEXT = (10, 12)
        UPPER, LOWER = slice(0, DH0), slice(DH0, 2 * DH0)
        A0_SPLITS = [s for s in A0_PIECES if A0_PIECES[s][0] != "out"]

        def a0_piece(s, first, last):
            piece = A0_PIECES.get(s)
            if piece is None or (first and piece[0] == "out" and piece[1] < 0) or (last and s in A0_NEXT):
                return None
            return piece

        def a0_splits(h, s, last):
            n = sum(1 for z in A0_SPLITS if z <= s and not (last and z in A0_NEXT))
            return h * len(A0_SPLITS) + (len(A0_NEXT) + n)

        def a0_outs(h, s):
            return h * 4 + (sum(1 for z in A0_PIECES if z <= s and A0_PIECES[z][0] == "out") - 2)

        def a0_bank_free(pe, h, s, first, last):
            z = s - 1
            while z >= 0 and a0_piece(z, first, last) is None:
                z -= 1
            if (z >= 0 and A0_PIECES[z][0] == "out") or (z < 0 and not first):
                pe.wait_ge(S["a0_out_added"], a0_outs(h, z))
            else:
                pe.wait_ge(S["a0_split_lo"], a0_splits(h, z, last))

        def first_bank(i):
            return ps_s[:, i % 4 // 2, i % 2, :]

        def a0_pe_split(pe, piece, ps_m=ps_m):
            kind, b, half = piece
            if kind == "v":
                for j in range(TPC):
                    k0 = b * SEQ + half * BANK + j * P
                    ins = pe.matmul(ps_m[:, j * P:(j + 1) * P], xT_f[:, k0:k0 + P], a0_wv[:, :], start=True, stop=True)
            else:
                x = slice(b * SEQ + half * BANK, b * SEQ + (half + 1) * BANK)
                pe.matmul(ps_m[:, :], a0_wqk_hi[:, :], xT_hi[:, x], start=True, stop=False)
                pe.matmul(ps_m[:, :], a0_wqk_hi[:, :], xT_lo[:, x], start=False, stop=False)
                ins = pe.matmul(ps_m[:, :], a0_wqk_lo[:, :], xT_hi[:, x], start=False, stop=True)
            ins.then_inc(S["a0_split_in"], 1)

        def a0_pe_out(pe, n, par):
            pe.wait_ge(S["a0_o_out"], n + 1)
            pe.matmul(ps_m[:, :], a0_wo[:, :], a0_o[par][:, :], start=True, stop=True).then_inc(S["a0_out_in"], 1)

        def a0_pe_turn(pe, g, q):
            pe.wait_ge(S["a0_p_normed"], g + 1)
            for half in range(2):
                pe.wait_ge(S["a0_pt_lo"], from0(2 * g + (half - 1)))
                for j in range(4):
                    k0 = (half * 4 + j) * P
                    ins = pe.transpose(ps_t[:, half, j * P:(j + 1) * P], a0_p[q % 4][:, k0:k0 + P], ident[:, :])
                ins.then_inc(S["a0_turned"], 1)

        def a0_pe_pv(pe, n, of_head, quarter):
            if quarter == 0:
                pe.wait_ge(S["a0_pt_lo"], 8 * n + 8)
                pe.wait_ge(S["a0_o_out"], n)
            b, par = of_head // 2, of_head % 2
            for kt in range(2 * quarter, 2 * quarter + 2):
                pe.matmul(ps_o[:, :], a0_v[b][:, kt, :], a0_pth[par][:, kt, :], start=kt == 0, stop=False)
                ins = pe.matmul(ps_o[:, :], a0_v[b][:, kt, :], a0_ptl[par][:, kt, :], start=False, stop=kt == KT - 1)
            if quarter == 3:
                ins.then_inc(S["a0_pv"], 1)

        def a0_pe(pe):
            pe.wait_ge(S["x_lo"], NC)
            pe.wait_ge(S["a0_w_lo"], 1)
            for i, s in enumerate(A0_NEXT):
                a0_pe_split(pe, A0_PIECES[s], first_bank(i))
            pe.wait_ge(S["a0_wv_loaded"], 16)

            def body(h, first, last):
                for s in range(SLOTS):
                    g = h * SLOTS + s
                    b, q = s // KT, s % KT
                    if s in (0, KT):
                        pe.wait_ge(S["a0_kh_copied"], 64 * h + (32 if s == 0 else 64))
                        pe.wait_ge(S["a0_kl_copied"], 64 * h + (32 if s == 0 else 64))
                    pe.wait_ge(S["a0_exped"], from0(g - 1))
                    for half in range(2):
                        k = slice(half * BANK, (half + 1) * BANK)
                        queries = a0_q[b][:, q * P:(q + 1) * P]
                        pe.matmul(ps_s[:, s % 2, half, :], queries, a0_kh[b][:, k], start=True, stop=False)
                        ins = pe.matmul(ps_s[:, s % 2, half, :], queries, a0_kl[b][:, k], start=False, stop=True)
                    ins.then_inc(S["a0_scores"], 1)
                    piece = a0_piece(s, first, last)
                    if piece is not None:
                        a0_bank_free(pe, h, s, first, last)
                        if piece[0] == "out":
                            if s == 11:
                                pe.wait_ge(S["a0_wo_loaded"], h * 16 + 16)
                            a0_pe_out(pe, h * 4 + piece[1], piece[1] % 2)
                        else:
                            if s == 2:
                                pe.wait_ge(S["a0_wv_loaded"], h * 16 + 16)
                            if s == A0_NEXT[0]:
                                pe.wait_ge(S["a0_w_lo"], h + 2)
                            a0_pe_split(pe, piece)
                    if not (first and s < 2):
                        a0_pe_turn(pe, g - 2, (s - 2) % SLOTS)
                    n, quarter = (s - 6) // 4, (s - 6) % 4
                    if not (first and n < 0):
                        if s in (6, 14):
                            pe.wait_ge(S["a0_split_lo"], a0_splits(h, s - 1, last))
                        a0_pe_pv(pe, h * 4 + n, n % 4, quarter)

            heads(pe, H0, body)
            g, n = H0 * SLOTS, H0 * 4
            for i in range(2):
                a0_pe_turn(pe, g - 2 + i, SLOTS - 2 + i)
                a0_pe_pv(pe, n - 2, 2, 2 + i)
            pe.wait_ge(S["a0_exped"], g)
            for c in range(2):
                y0_turn(pe, c)
            for quarter in range(4):
                a0_pe_pv(pe, n - 1, 3, quarter)
                if quarter == 1:
                    pe.wait_ge(S["a0_out_added"], n - 2)
                    a0_pe_out(pe, n - 2, 0)
            pe.wait_ge(S["a0_out_added"], n - 1)
            a0_pe_out(pe, n - 1, 1)

        def a0_act_split(act, count, piece, ps_m=ps_m):
            kind, b, half = piece
            cols = slice(half * BANK, (half + 1) * BANK)
            act.wait_ge(S["a0_split_in"], count)
            if kind == "v":
                src = ps_m[:, :].rearrange("p (t c) -> p t c", c=P)[:, :, 0:DH0]
                ins = act.activation(a0_v[b][:, half * TPC:(half + 1) * TPC, 0:DH0], src, ACT.Copy)
            else:
                act.activation(a0_q[b][UPPER, cols], ps_m[UPPER, :], ACT.Copy, scale=DH0 ** -0.5)
                ins = act.activation(a0_kh[b][LOWER, cols], ps_m[LOWER, :], ACT.Copy)
            ins.then_inc(S["a0_split_hi"], 1)

        def a0_dve_split(dve, count, piece, ps_m=ps_m):
            kind, b, half = piece
            cols = slice(half * BANK, (half + 1) * BANK)
            dve.wait_ge(S["a0_split_hi"], count)
            if kind == "v":
                src = ps_m[:, :].rearrange("p (t c) -> p t c", c=P)[:, :, DH0:2 * DH0]
                v = a0_v[b][:, half * TPC:(half + 1) * TPC, :]
                ins = dve.tensor_tensor(v[:, :, DH0:2 * DH0], src, v[:, :, 0:DH0], ALU.subtract)
            else:
                dve.scalar_tensor_tensor(out=a0_q[b][LOWER, cols], in0=ps_m[UPPER, :], scalar=DH0 ** -0.5,
                                         in1=a0_q[b][UPPER, cols], op0=ALU.mult, op1=ALU.subtract)
                ins = dve.tensor_tensor(a0_kl[b][LOWER, cols], ps_m[LOWER, :], a0_kh[b][LOWER, cols], ALU.subtract)
            ins.then_inc(S["a0_split_lo"], 1)

        def a0_pt_part(q, half):
            return slice(None), slice(half * 4, half * 4 + 4), slice((q % 4) * P, (q % 4 + 1) * P)

        def a0_act(act):
            for i, s in enumerate(A0_NEXT):
                a0_act_split(act, i + 1, A0_PIECES[s], first_bank(i))

            def pt_hi(g, q):
                for half in range(2):
                    act.wait_ge(S["a0_turned"], 2 * g + (half + 1))
                    act.activation(a0_pth[(q // 4) % 2][a0_pt_part(q, half)],
                                   ps_t[:, half, :].rearrange("p (t c) -> p t c", c=P), ACT.Copy)\
                        .then_inc(S["a0_pt_hi"], 1)

            def o_out(n, par):
                act.wait_ge(S["a0_pv"], n + 1)
                act.wait_ge(S["a0_out_in"], from0(n - 1))
                act.activation(a0_o[par][:, :], ps_o[:, :], ACT.Copy).then_inc(S["a0_o_out"], 1)

            def body(h, first, last):
                for s in range(SLOTS):
                    g = h * SLOTS + s
                    if s % 4 == 2 and not (first and s < 10):
                        o_out(h * 4 + (s - 10) // 4, (s - 10) // 4 % 2)
                    piece = a0_piece(s, first, last)
                    if piece is not None and piece[0] != "out":
                        a0_act_split(act, a0_splits(h, s, last), piece)
                    if not (first and s < 2):
                        q = (s - 2) % SLOTS
                        if q % 4 == 0:
                            act.wait_ge(S["a0_pv"], from0(h * 4 + ((s - 2) // 4 - 1)))
                        pt_hi(g - 2, q)
                    act.wait_ge(S["a0_negmaxed"], g + 1)
                    act.wait_ge(S["a0_turned"], from0(2 * g - 6))
                    act.activation(a0_p[s % 4][:, :], ps_s[:, s % 2, :, :], ACT.Exp, bias=a0_negmax[:, s % 4:s % 4 + 1],
                                   accum_out=a0_sum[:, s % 4:s % 4 + 1]).then_inc(S["a0_exped"], 1)

            heads(act, H0, body)
            g, n = H0 * SLOTS, H0 * 4
            pt_hi(g - 2, SLOTS - 2)
            pt_hi(g - 1, SLOTS - 1)
            o_out(n - 2, 0)
            o_out(n - 1, 1)

        def a0_dve(dve):
            for i, s in enumerate(A0_NEXT):
                a0_dve_split(dve, i + 1, A0_PIECES[s], first_bank(i))

            def pt_lo(g, q):
                for half in range(2):
                    dve.wait_ge(S["a0_pt_hi"], 2 * g + (half + 1))
                    at = a0_pt_part(q, half)
                    dve.tensor_tensor(a0_ptl[(q // 4) % 2][at], ps_t[:, half, :].rearrange("p (t c) -> p t c", c=P),
                                      a0_pth[(q // 4) % 2][at], ALU.subtract).then_inc(S["a0_pt_lo"], 1)

            def add_out(n, of_head):
                dve.wait_ge(S["a0_out_in"], n + 1)
                dve.wait_ge(S["a0_out_added"], n)
                y = Yflat[:, of_head * BANK:(of_head + 1) * BANK]
                dve.tensor_tensor(y, ps_m[:, :], y, ALU.add).then_inc(S["a0_out_added"], 1)

            def rsum(g, s):
                col = slice(s % 4, s % 4 + 1)
                dve.wait_ge(S["a0_exped"], g + 1)
                dve.wait_ge(S["a0_p_normed"], from0(g - 3))
                dve.reciprocal(a0_rsum[:, col], a0_sum[:, col]).then_inc(S["a0_rsummed"], 1)

            def body(h, first, last):
                for s in range(SLOTS):
                    g = h * SLOTS + s
                    dve.wait_ge(S["a0_scores"], g + 1)
                    dve.tensor_reduce(a0_negmax[:, s % 4:s % 4 + 1], ps_s[:, s % 2, :, :], AX.XY, ALU.max, negate=True)\
                        .then_inc(S["a0_negmaxed"], 1)
                    if not (first and s < 1):
                        rsum(g - 1, (s - 1) % SLOTS)
                    piece = a0_piece(s, first, last)
                    if piece is not None and piece[0] == "out":
                        add_out(h * 4 + piece[1], piece[1] % 4)
                    elif piece is not None:
                        a0_dve_split(dve, a0_splits(h, s, last), piece)
                    if not (first and s < 2):
                        pt_lo(g - 2, (s - 2) % SLOTS)

            heads(dve, H0, body)
            g, n = H0 * SLOTS, H0 * 4
            rsum(g - 1, SLOTS - 1)
            pt_lo(g - 2, SLOTS - 2)
            pt_lo(g - 1, SLOTS - 1)
            dve.wait_ge(S["y0_turned"], 2)
            y0_norm(dve, 0, 0)
            add_out(n - 2, 2)
            y0_norm(dve, 1, 0)
            y0_norm(dve, 2, 0)
            add_out(n - 1, 3)

        def a0_pool(pool):
            def weights(h):
                pool.wait_ge(S["a0_wqk_loaded"], h * 16 + 16)
                pool.sem_inc(S["waited"], 1)
                pool.tensor_scalar(a0_wqk_hi[:, :], a0_wqk_raw[:, :], 1.0, 0.0, ALU.mult, ALU.add)\
                    .then_inc(S["a0_w_hi"], 1)
                pool.wait_ge(S["a0_w_hi"], h + 1)
                pool.tensor_tensor(a0_wqk_lo[:, :], a0_wqk_raw[:, :], a0_wqk_hi[:, :], ALU.subtract)\
                    .then_inc(S["a0_w_lo"], 1)

            weights(0)

            def scale(g, s):
                pool.wait_ge(S["a0_rsummed"], g + 1)
                pool.sem_inc(S["waited"], 1)
                pool.tensor_scalar(a0_p[s % 4][:, :], a0_p[s % 4][:, :], a0_rsum[:, s % 4:s % 4 + 1], 1.0,
                                   ALU.mult, ALU.mult).then_inc(S["a0_p_normed"], 1)

            def body(h, first, last):
                for s in range(SLOTS):
                    g = h * SLOTS + s
                    if s == 7 and not last:
                        pool.wait_ge(S["a0_split_in"], a0_splits(h, 4, last))
                        weights(h + 1)
                    if not (first and s < 1):
                        scale(g - 1, (s - 1) % SLOTS)

            heads(pool, H0, body)
            scale(H0 * SLOTS - 1, SLOTS - 1)

        def a0_load_first(sp):
            sp.dma_start(a0_wqk_raw[:, :], t["l0_wqk"][0]).then_inc(S["a0_wqk_loaded"], 16)
            sp.dma_start(a0_wv[:, :], t["l0_wv"][0]).then_inc(S["a0_wv_loaded"], 16)

        def f0_load_early(sp):
            for e in range(NE):
                sp.dma_start(f0_w1_raw[:, e, :], t["ffn0_w1"][:, e, :]).then_inc(S["f0_w1_loaded"][e], 16)

        def a0_copy_k(sp, m, split, piece, prologue=False):
            _, b, half = piece
            cols = slice(half * BANK, (half + 1) * BANK)
            sp.wait_ge(S["a0_split_lo"], split)
            if not prologue:
                sp.wait_ge(S["a0_kh_copied"], m * 16)
                sp.wait_ge(S["a0_kl_copied"], m * 16)
            sp.dma_start(a0_kh[b][UPPER, cols].bitcast(F32), a0_kh[b][LOWER, cols].bitcast(F32)).then_inc(S["a0_kh_copied"], 16)
            sp.dma_start(a0_kl[b][UPPER, cols].bitcast(F32), a0_kl[b][LOWER, cols].bitcast(F32)).then_inc(S["a0_kl_copied"], 16)

        def a0_sp(sp):
            for i, s in enumerate(A0_NEXT):
                a0_copy_k(sp, i, i + 1, A0_PIECES[s], prologue=True)
            f0_load_early(sp)

            def body(h, first, last):
                if not last:
                    sp.wait_ge(S["a0_w_lo"], h + 1)
                    sp.dma_start(a0_wqk_raw[:, :], row(t["l0_wqk"], h + 1)).then_inc(S["a0_wqk_loaded"], 16)
                m = 4 * h + 2
                for s in (0, 4):
                    a0_copy_k(sp, m, a0_splits(h, s, last), A0_PIECES[s])
                    m = m + 1
                sp.wait_ge(S["a0_out_in"], h * 4)
                sp.dma_start(a0_wo[:, :], row(t["l0_wo"], h)).then_inc(S["a0_wo_loaded"], 16)
                if not last:
                    for s in A0_NEXT:
                        a0_copy_k(sp, m, a0_splits(h, s, last), A0_PIECES[s])
                        m = m + 1
                    sp.wait_ge(S["a0_split_in"], a0_splits(h, 13, last))
                    sp.dma_start(a0_wv[:, :], row(t["l0_wv"], h + 1)).then_inc(S["a0_wv_loaded"], 16)

            heads(sp, H0, body)

        def y0_bank(c):
            return ps_s[:, c // 2, c % 2, :]

        def y0_turn(pe, c):
            pe.wait_ge(S["a0_out_added"], 4 * (H0 - 1) + c + 1)
            for i in range(TPC):
                ins = pe.transpose(y0_bank(c)[:, i * P:(i + 1) * P], Yflat[:, (c * TPC + i) * P:(c * TPC + i + 1) * P],
                                   ident[:, :])
            ins.then_inc(S["y0_turned"], 1)

        def y0_norm(dve, stage, pair):
            norm_pair(dve, stage, NORM_A0 + 4 * pair, 2 * pair, lambda i, k: bank_tile(y0_bank(2 * pair + i), k))

        def f0_pre_pe(pe):
            y0_turn(pe, 2)
            y0_turn(pe, 3)
            for c in range(NC):
                pe.wait_ge(S["xst_ready"], NC + c + 1)
                turn_pe(pe, TURN_A0 + c, c, lambda i: xst[c % 2][:, i, :])
                if c:
                    logits_pe(pe, c - 1)
            logits_pe(pe, NC - 1)
            pe.wait_ge(S["f0_comb_ready"], 1)
            for i in range(NT):
                ins = pe.transpose(ps_s[0:NE, i // 8, i // 4 % 2, (i % 4) * P:(i % 4 + 1) * P], f0_comb[:, i, :],
                                   ident[:, :])
            ins.then_inc(S["f0_combT_in"], 1)
            pe.wait_ge(S["f0_combT_ready"], 1)
            pe.wait_ge(S["f0_small_loaded"], 16 * 4)
            for i in range(NT):
                ins = pe.matmul(ps_s[:, i // 8, i // 4 % 2, (i % 4) * P:(i % 4 + 1) * P],
                                f0_combT[:, i * P:(i + 1) * P], f0_b2[:, :], start=True, stop=True)
            ins.then_inc(S["f0_bias_in"], 1)

        def logits_pe(pe, c):
            pe.wait_ge(S["f0_nT_ready"], c + 1)
            for i in range(TPC):
                k = (c * TPC + i) * NR
                ins = pe.matmul(ps_m[:, k:k + NR], f0_nT[c % 2][:, i * P:(i + 1) * P], f0_rw[:, :], start=True, stop=True)
            ins.then_inc(S["f0_logits"], 1)

        def f0_pre_act(act):
            act.wait_ge(S["a0_out_added"], 4 * H0)
            act.wait_ge(S["f0_small_loaded"], 16 * 4)

            def w1_hi(e):
                act.wait_ge(S["f0_w1_loaded"][e], 16)
                act.activation(f0_w1_hi[:, e, :], f0_w1_raw[:, e, :], ACT.Copy).then_inc(S["f0_w1_hi_ready"], 1)

            for c in range(NC):
                if c in (0, 2):
                    for e in range(4 * (c // 2), 4 * (c // 2) + 4):
                        w1_hi(e)
                act.wait_ge(S["x_turned"], TURN_A0 + c + 1)
                act.wait_ge(S["f0_logits"], from0(c - 1))
                act.activation(f0_nT[c % 2][:, :], ps_t[:, c % 2, :], ACT.Copy, scale=f0_nw[:, 0:1])\
                    .then_inc(S["f0_nT_ready"], 1)
                turn_act(act, TURN_A0 + c, c, scale=f0_nw[:, 0:1])
            act.wait_ge(S["f0_logits"], NC)
            act.activation(f0_prob[:, :, :], ps_m[:, 0:NT * NR].rearrange("p (t e) -> p t e", e=NR), ACT.Exp,
                           scale=-1.0).then_inc(S["f0_exped"], 1)
            w1_hi(NE - 1)
            act.wait_ge(S["f0_combT_in"], 1)
            act.activation(f0_combT[:, :], ps_s[0:NE, :, :, :], ACT.Copy).then_inc(S["f0_combT_ready"], 1)
            act.wait_ge(S["f0_bias_in"], 1)
            act.activation(Y[:, :, :], ps_s[:, :, :, :], ACT.Copy).then_inc(S["f0_y_started"], 1)

        def f0_pre_dve(dve):
            for e in range(NR):
                ins = dve.memset(f0_rank[:, e:e + 1], float(NR - e))
            ins.then_inc(S["dve_step"], 1)
            dve.wait_ge(S["dve_step"], dve_steps.next())
            dve.sem_inc(S["waited"], 1)
            y0_norm(dve, 3, 0)
            dve.wait_ge(S["y0_turned"], 4)
            y0_norm(dve, 0, 1)
            y0_norm(dve, 4, 0)
            dve.wait_ge(S["x_turned"], TURN_A0 + 2)
            y0_norm(dve, 1, 1)
            y0_norm(dve, 2, 1)
            turn_dve(dve, TURN_A0, 0, f0_nT[0][:, :])
            y0_norm(dve, 3, 1)
            turn_dve(dve, TURN_A0 + 1, 1, f0_nT[1][:, :])
            y0_norm(dve, 4, 1)
            for c in range(2, NC):
                turn_dve(dve, TURN_A0 + c, c, f0_nT[c % 2][:, :])

            def step(ins):
                ins.then_inc(S["dve_step"], 1)
                dve.wait_ge(S["dve_step"], dve_steps.next())

            over_e = lambda ap: ap[:, :].rearrange("p (t a) -> p t a", a=1).broadcast_to([P, NT, NR])
            rank = f0_rank[:, :].rearrange("p (a e) -> p a e", a=1).broadcast_to([P, NT, NR])
            dve.wait_ge(S["f0_exped"], 1)
            step(dve.tensor_scalar(f0_tmp[:, :, :], f0_prob[:, :, :], 1.0, None, ALU.add))
            step(dve.reciprocal(f0_prob[:, :, :], f0_tmp[:, :, :]))
            for k, p in ((0, f0_prob), (1, f0_left)):
                step(dve.tensor_reduce(f0_top[k][:, :], p[:, :, :], AX.X, ALU.max))
                step(dve.tensor_tensor(f0_tmp[:, :, :], p[:, :, :], over_e(f0_top[k]), ALU.is_equal))
                step(dve.tensor_tensor(f0_tmp2[:, :, :], f0_tmp[:, :, :], rank, ALU.mult))
                step(dve.tensor_reduce(f0_idx[:, :], f0_tmp2[:, :, :], AX.X, ALU.max))
                step(dve.tensor_tensor(f0_one[k][:, :, :], f0_tmp2[:, :, :], over_e(f0_idx), ALU.is_equal))
                if k == 0:
                    step(dve.scalar_tensor_tensor(out=f0_left[:, :, :], in0=f0_one[0][:, :, :], scalar=-4.0,
                                                  in1=f0_prob[:, :, :], op0=ALU.mult, op1=ALU.add))
            step(dve.tensor_tensor(f0_den[:, :], f0_top[0][:, :], f0_top[1][:, :], ALU.add))
            step(dve.tensor_scalar(f0_den[:, :], f0_den[:, :], EPS_TOPK, None, ALU.add))
            step(dve.reciprocal(f0_idx[:, :], f0_den[:, :]))
            for k in range(2):
                step(dve.tensor_tensor(f0_top[k][:, :], f0_top[k][:, :], f0_idx[:, :], ALU.mult))
                step(dve.tensor_tensor(f0_one[k][:, :, :], f0_one[k][:, :, :], over_e(f0_top[k]), ALU.mult))
            dve.memset(f0_comb[:, :, NR:NE], 1.0)
            dve.tensor_tensor(f0_comb[:, :, 0:NR], f0_one[0][:, :, :], f0_one[1][:, :, :], ALU.add)\
                .then_inc(S["f0_comb_ready"], 1)

        def f0_pre_pool(pool):
            for pair in range(2):
                for k in range(2):
                    norm_rstd(pool, NORM_A0 + 4 * pair + k, 2 * pair + k)
                for k in range(2):
                    norm_rstd_rms(pool, NORM_A0 + 4 * pair + 2 + k, 2 * pair + k)
            for e in range(NE):
                pool.wait_ge(S["f0_w1_hi_ready"], e + 1)
                pool.tensor_tensor(f0_w1_lo[:, e, :], f0_w1_raw[:, e, :], f0_w1_hi[:, e, :], ALU.subtract)\
                    .then_inc(S["f0_w1_lo_ready"], 1)

        def f0_sp(sp):
            sp.wait_ge(S["a0_out_added"], 4 * H0)
            for dst, name in ((f0_rw, "ffn0_rw"), (f0_nw, "ffn0_nw"), (f0_b2, "ffn0_b2")):
                sp.dma_start(dst[:, :], t[name]).then_inc(S["f0_small_loaded"], 16)
            sp.dma_start(f0_b1[:, :, :], t["ffn0_b1"]).then_inc(S["f0_small_loaded"], 16)
            sp.dma_start(f0_w2[:, :, :, :], t["ffn0_w2"]).then_inc(S["f0_w2_loaded"], 16)

        def f0_pe(pe):
            pe.wait_ge(S["f0_w2_loaded"], 16)
            pe.wait_ge(S["x_lo"], TURN_F0)
            pe.wait_ge(S["f0_y_started"], 1)
            with pe.Fori(0, NC) as c:
                x = bass.ds(c * BANK, BANK)

                def up(e):
                    pe.wait_ge(S["f0_w1_lo_ready"], e + 1)
                    for ht in range(HT):
                        if e == 0:
                            pe.wait_ge(S["f0_relued"], c * (NE * HT))
                        else:
                            pe.wait_ge(S["f0_relued"], from0(c * (NE * HT) + (HT * e + ht - 3)))
                        bank = ps_s[:, ht // 2, ht % 2, :]
                        w = slice(ht * P, (ht + 1) * P)
                        pe.matmul(bank, f0_w1_hi[:, e, w], xT_hi[:, x], start=True, stop=False)
                        pe.matmul(bank, f0_w1_hi[:, e, w], xT_lo[:, x], start=False, stop=False)
                        pe.matmul(bank, f0_w1_lo[:, e, w], xT_hi[:, x], start=False, stop=True)\
                            .then_inc(S["f0_up"], 1)

                def down(e):
                    pe.wait_ge(S["f0_relued"], c * (NE * HT) + HT * (e + 1))
                    pe.wait_ge(S["f0_added"], from0(c * NE + max(e - 1, 0)))
                    for i in range(TPC):
                        for ht in range(HT):
                            ins = pe.matmul(ps_t[:, e % 2, i * P:(i + 1) * P], f0_h[e % 2][ht][:, i * P:(i + 1) * P],
                                            f0_w2[:, e, ht, :], start=ht == 0, stop=ht == HT - 1)
                    ins.then_inc(S["f0_down"], 1)

                for e in range(NE):
                    up(e)
                    if e:
                        down(e - 1)
                down(NE - 1)

        def f0_act(act):
            with act.Fori(0, NC) as c:
                for e in range(NE):
                    for ht in range(HT):
                        act.wait_ge(S["f0_up"], c * (NE * HT) + (HT * e + ht + 1))
                        if ht == 0:
                            act.wait_ge(S["f0_down"], from0(c * NE + max(e - 1, 0)))
                        act.activation(f0_h[e % 2][ht][:, :], ps_s[:, ht // 2, ht % 2, :], ACT.Relu,
                                       bias=f0_b1[:, e, ht:ht + 1]).then_inc(S["f0_relued"], 1)

        def f0_dve(dve):
            dve.wait_ge(S["f0_y_started"], 1)

            def add_experts(c):
                for e in range(NE):
                    dve.wait_ge(S["f0_down"], c * NE + (e + 1))
                    dve.wait_ge(S["f0_added"], c * NE + e)
                    for i in range(TPC):
                        y = Y[:, bass.ds(c * TPC + i, 1), :]
                        w = f0_comb[:, bass.ds(c * TPC + i, 1), e:e + 1].rearrange("p a b -> p (a b)")
                        ins = dve.scalar_tensor_tensor(out=y, in0=bank_tile(ps_t[:, e % 2, :], i), scalar=w, in1=y,
                                                       op0=ALU.mult, op1=ALU.add)
                    ins.then_inc(S["f0_added"], 1)
                dve.wait_ge(S["f0_added"], c * NE + NE)
                dve.sem_inc(S["waited"], 1)

            y_of = lambda c: lambda i: Y[:, bass.ds(c * TPC + i, 1), :]
            with dve.Fori(0, NC - 1) as c:
                dve_steps.enter(c, 4)
                add_experts(c)
                add_and_norm(dve, c * 2 + NORM_F0, c, y_of(c), y_of(c)).then_inc(S["x1_ready"], 1)
                dve_steps.leave(NC - 1)

            def step(ins):
                ins.then_inc(S["dve_step"], 1)
                dve.wait_ge(S["dve_step"], dve_steps.next())

            c, n = NC - 1, NORM_F0 + 2 * (NC - 1)
            add_experts(c)
            dve.wait_ge(S["a1_lam_loaded"], 16)
            lam = a1_lam[:, :, :].rearrange("p (m w) h -> p m w h", w=2)
            dve.tensor_tensor(a1_lprod[:, :, :], lam[:, :, 0, :], lam[:, :, 1, :], ALU.mult)\
                .then_inc(S["a1_lprod_ready"], 1)
            norm_stats(dve, n, 0, y_of(c))
            turn_dve(dve, TURN_F0, 0, ps_t[:, 0, :])
            step(norm_apply(dve, n, 0, y_of(c), lambda i: tile(xhat, i)))
            xc = X[:, c * TPC:(c + 1) * TPC, :]
            step(dve.tensor_tensor(xc, xc, xhat[:, :, :], ALU.add))
            x_tile = lambda i: tile(X, c * TPC + i)
            norm_stats(dve, n + 1, 1, x_tile)
            turn_dve(dve, TURN_F0 + 1, 1, ps_t[:, 1, :])
            norm_apply(dve, n + 1, 1, x_tile, y_of(c)).then_inc(S["x1_ready"], 1)
            turn_dve(dve, TURN_F0 + 2, 2, ps_t[:, 0, :])
            dve.wait_ge(S["a1_lexped"], 1)
            step(dve.tensor_tensor(a1_neglam[:, :], a1_lexp[:, 1, :], a1_lexp[:, 0, :], ALU.subtract))
            step(dve.tensor_scalar(a1_neglam[:, :], a1_neglam[:, :], -LAMBDA_INIT, None, ALU.add))

        def f0_pool(pool):
            for b in range(B):
                a1_weights(pool, b + 1, 0, b)
            with pool.Fori(0, NC) as c:
                pool_steps.enter(c, 2)
                norm_rstd(pool, c * 2 + NORM_F0, 0)
                norm_rstd(pool, c * 2 + (NORM_F0 + 1), 1)
                pool_steps.leave(NC)

        Q1, Q2, K1, K2, V = range(5)
        HALF_BODY = [[(K1, 0)], [(K1, 1), (V, 0)], [(Q1, 0), (V, 1)], [(Q1, 1), (V, 2)],
                     [(K2, 0), (V, 3)], [(K2, 1)], [(Q2, 0)], [(Q2, 1)]]
        A1_FIRST = [piece for slot in HALF_BODY for piece in slot]
        NP1 = len(A1_FIRST)
        A1_TURN_AFTER = 5

        def a1_pieces(s, last):
            if last and s >= KT:
                return []
            return [(kind, 1 if s < KT else 0, half) for kind, half in HALF_BODY[s % KT]]

        def a1_splits(h, s, last, of_slot=99):
            n = sum(len(a1_pieces(z, last)) for z in range(s)) + min(of_slot, len(a1_pieces(s, last)) if s >= 0 else 0)
            return h * (2 * NP1) + (NP1 + n)

        def a1_pe_piece(pe, piece, ps_m=ps_m):
            kind, b, half = piece
            if kind == V:
                w = slice(4 * DH1, 4 * DH1 + DV1)
                for j in range(2):
                    k0 = b * SEQ + (half * 2 + j) * P
                    dst = ps_m[:, j * DV1:(j + 1) * DV1]
                    pe.matmul(dst, xT_hi[:, k0:k0 + P], a1_w_hi[b][:, w], start=True, stop=False)
                    pe.matmul(dst, xT_hi[:, k0:k0 + P], a1_w_lo[b][:, w], start=False, stop=False)
                    ins = pe.matmul(dst, xT_lo[:, k0:k0 + P], a1_w_hi[b][:, w], start=False, stop=True)
            else:
                w = slice(kind * DH1, (kind + 1) * DH1)
                x = slice(b * SEQ + half * BANK, b * SEQ + (half + 1) * BANK)
                pe.matmul(ps_m[:, :], a1_w_hi[b][:, w], xT_hi[:, x], start=True, stop=False)
                pe.matmul(ps_m[:, :], a1_w_hi[b][:, w], xT_lo[:, x], start=False, stop=False)
                ins = pe.matmul(ps_m[:, :], a1_w_lo[b][:, w], xT_hi[:, x], start=False, stop=True)
            ins.then_inc(S["a1_split_in"], 1)

        def a1_piece_parts(piece, ps_m):
            kind, b, half = piece
            if kind == V:
                tiles = slice(2 * half, 2 * half + 2)
                return (a1_vh[b][:, tiles, :], a1_vl[b][:, tiles, :],
                        ps_m[:, :].rearrange("p (t c) -> p t c", t=2), 1.0)
            cols = slice(half * BANK, (half + 1) * BANK)
            return (a1_hi[b][kind][:, cols], a1_lo[b][kind][:, cols], ps_m[:, :],
                    DH1 ** -0.5 if kind in (Q1, Q2) else 1.0)

        def a1_act_piece(act, count, piece, ps_m=ps_m):
            hi, lo, src, scale = a1_piece_parts(piece, ps_m)
            act.wait_ge(S["a1_split_in"], count)
            act.activation(hi, src, ACT.Copy, scale=scale).then_inc(S["a1_split_hi"], 1)

        def a1_dve_piece(dve, count, piece, ps_m=ps_m):
            hi, lo, src, scale = a1_piece_parts(piece, ps_m)
            dve.wait_ge(S["a1_split_hi"], count)
            if scale == 1.0:
                ins = dve.tensor_tensor(lo, src, hi, ALU.subtract)
            else:
                ins = dve.scalar_tensor_tensor(out=lo, in0=src, scalar=scale, in1=hi, op0=ALU.mult, op1=ALU.subtract)
            ins.then_inc(S["a1_split_lo"], 1)

        def a1_pe_scores(pe, g, b, q, m):
            pe.wait_ge(S["a1_exped"], from0(2 * g + (m - 1)))
            for half in range(2):
                k = slice(half * BANK, (half + 1) * BANK)
                qs = slice(q * P, (q + 1) * P)
                dst = ps_s[:, m, half, :]
                pe.matmul(dst, a1_hi[b][Q1 + m][:, qs], a1_hi[b][K1 + m][:, k], start=True, stop=False)
                pe.matmul(dst, a1_hi[b][Q1 + m][:, qs], a1_lo[b][K1 + m][:, k], start=False, stop=False)
                ins = pe.matmul(dst, a1_lo[b][Q1 + m][:, qs], a1_hi[b][K1 + m][:, k], start=False, stop=True)
            ins.then_inc(S["a1_scores"], 1)

        def a1_pe_turn(pe, g, par):
            pe.wait_ge(S["a1_combined"], g + 1)
            for half in range(2):
                pe.wait_ge(S["a1_pt_lo"], from0(2 * g + (half - 1)))
                for j in range(4):
                    k0 = (half * 4 + j) * P
                    ins = pe.transpose(ps_t[:, half, j * P:(j + 1) * P], a1_p[par][0][:, k0:k0 + P], ident[:, :])
                ins.then_inc(S["a1_turned"], 1)

        def a1_pe_pv(pe, g, b, keys):
            for kt in keys:
                if kt == 0:
                    pe.wait_ge(S["a1_o_normed"], g)
                if kt % 4 == 0:
                    pe.wait_ge(S["a1_pt_lo"], 2 * g + (kt // 4 + 1))
                dst = ps_o[:, 0:DV1]
                pe.matmul(dst, a1_ath[:, kt, :], a1_vh[b][:, kt, :], start=kt == 0, stop=False)
                pe.matmul(dst, a1_ath[:, kt, :], a1_vl[b][:, kt, :], start=False, stop=False)
                ins = pe.matmul(dst, a1_atl[:, kt, :], a1_vh[b][:, kt, :], start=False, stop=kt == KT - 1)
            if kt == KT - 1:
                ins.then_inc(S["a1_pv"], 1)

        def a1_pe_turn_o(pe, g, par):
            pe.wait_ge(S["a1_o_normed"], g + 1)
            pe.wait_ge(S["a1_added"], g)
            for j in range(2):
                ins = pe.transpose(ps_m[:, j * P:(j + 1) * P], a1_on[par][:, j * P:(j + 1) * P], ident[:, :])
            ins.then_inc(S["a1_ot_in"], 1)

        def a1_pe_out(pe, g, par, b):
            pe.wait_ge(S["a1_ot_out"], g + 1)
            for j in range(2):
                ins = pe.matmul(ps_m[:, 2 * P:3 * P], a1_ot[par][:, j * P:(j + 1) * P], a1_wo[b][:, j, :],
                                start=j == 0, stop=j == 1)
            ins.then_inc(S["a1_out_in"], 1)

        def a1_pe(pe):
            pe.wait_ge(S["f0_added"], NC * NE)
            pe.wait_ge(S["a1_lprod_ready"], 1)
            pe.matmul(ps_o[:, 0:2 * H1], ones[:, :], a1_lprod[:, :, :], start=True, stop=True)\
                .then_inc(S["a1_lsum_in"], 1)

            def turn(c):
                pe.wait_ge(S["x1_ready"], c + 1)
                turn_pe(pe, TURN_F0 + c, c, lambda i: Y[:, c * TPC + i, :])

            for c in range(NC - 1):
                turn(c)
            pe.wait_ge(S["a1_w_lo"], 1)
            for i, (kind, half) in enumerate(A1_FIRST):
                if i == 0:
                    pe.wait_ge(S["x_lo"], TURN_F0 + 2)
                pe.wait_ge(S["a1_split_lo"], from0(i - 3))
                a1_pe_piece(pe, (kind, 0, half), first_bank(i))
                if i == A1_TURN_AFTER:
                    turn(NC - 1)
            pe.wait_ge(S["x_lo"], TURN_F0 + NC)
            pe.wait_ge(S["a1_lexped"], 1)

            def body(h, first, last):
                for s in range(SLOTS):
                    g = h * SLOTS + s
                    b, q = s // KT, s % KT
                    if s % KT == 0:
                        pe.wait_ge(S["a1_split_lo"], a1_splits(h, s - 1, last))
                    a1_pe_scores(pe, g, b, q, 0)
                    v_of = ((s - 2) % SLOTS) // KT
                    if not (first and s < 2):
                        a1_pe_pv(pe, g - 2, v_of, range(0, 4))
                    if not (first and s < 3):
                        pe.wait_ge(S["a1_split_lo"], a1_splits(h, s - 1, last))
                        a1_pe_turn_o(pe, g - 3, (s - 3) % 2)
                    if not (first and s < 2):
                        a1_pe_pv(pe, g - 2, v_of, range(4, 6))
                    if not (first and s < 3):
                        if s == 3 or s == KT + 3:
                            pe.wait_ge(S["a1_wo_scaled"], 2 * h + (1 + b))
                        a1_pe_out(pe, g - 3, (s - 3) % 2, ((s - 3) % SLOTS) // KT)
                    if not (first and s < 2):
                        a1_pe_pv(pe, g - 2, v_of, range(6, 8))
                    pieces = a1_pieces(s, last)
                    if s % KT == 0 and pieces:
                        pe.wait_ge(S["a1_w_lo"], 2 * h + (2 if s == 0 else 3))
                    if pieces:
                        pe.wait_ge(S["a1_added"], from0(g - 2))
                        pe.wait_ge(S["a1_split_lo"], a1_splits(h, s - 1, last))
                        a1_pe_piece(pe, pieces[0])
                    a1_pe_scores(pe, g, b, q, 1)
                    if not (first and s < 1):
                        a1_pe_turn(pe, g - 1, (s - 1) % 2)
                    if len(pieces) > 1:
                        pe.wait_ge(S["a1_split_lo"], a1_splits(h, s, last, 1))
                        a1_pe_piece(pe, pieces[1])

            heads(pe, H1, body)
            g = H1 * SLOTS
            a1_pe_pv(pe, g - 2, 1, range(0, 4))
            a1_pe_turn_o(pe, g - 3, 1)
            a1_pe_turn(pe, g - 1, 1)
            a1_pe_out(pe, g - 3, 1, 1)
            a1_pe_pv(pe, g - 2, 1, range(4, 8))
            a1_pe_turn_o(pe, g - 2, 0)
            a1_pe_pv(pe, g - 1, 1, range(0, 4))
            a1_pe_out(pe, g - 2, 0, 1)
            a1_pe_pv(pe, g - 1, 1, range(4, 8))
            a1_pe_turn_o(pe, g - 1, 1)
            a1_pe_out(pe, g - 1, 1, 1)

        def a1_act(act):
            act.wait_ge(S["a1_lsum_in"], 1)
            act.activation(a1_lexp[:, :, :], ps_o[:, 0:2 * H1].rearrange("p (m h) -> p m h", m=2), ACT.Exp)\
                .then_inc(S["a1_lexped"], 1)
            for c in range(NC - 1):
                turn_act(act, TURN_F0 + c, c)
            for i, (kind, half) in enumerate(A1_FIRST):
                a1_act_piece(act, i + 1, (kind, 0, half), first_bank(i))
                if i == A1_TURN_AFTER:
                    turn_act(act, TURN_F0 + NC - 1, NC - 1)

            def at_hi(g):
                act.wait_ge(S["a1_pv"], g)
                for half in range(2):
                    act.wait_ge(S["a1_turned"], 2 * g + (half + 1))
                    act.activation(a1_ath[:, half * 4:half * 4 + 4, :],
                                   ps_t[:, half, :].rearrange("p (t c) -> p t c", c=P), ACT.Copy)\
                        .then_inc(S["a1_pt_hi"], 1)

            def ot_out(g, par):
                act.wait_ge(S["a1_ot_in"], g + 1)
                act.activation(a1_ot[par][:, :], ps_m[:, 0:2 * P], ACT.Copy).then_inc(S["a1_ot_out"], 1)

            def softmax(g, par, m):
                act.wait_ge(S["a1_negmaxed"], 2 * g + (m + 1))
                act.activation(a1_p[par][m][:, :], ps_s[:, m, :, :], ACT.Exp, bias=a1_negmax[:, par, m:m + 1],
                               accum_out=a1_sum[:, par, m:m + 1]).then_inc(S["a1_exped"], 1)

            def norm_o(g, par):
                act.wait_ge(S["a1_rms_ready"], g + 1)
                act.wait_ge(S["a1_ot_in"], from0(g - 1))
                act.activation(a1_on[par][:, :], ps_o[:, 0:DV1], ACT.Copy, scale=a1_r[:, par:par + 1])\
                    .then_inc(S["a1_o_normed"], 1)

            def sum_square(g, par):
                act.wait_ge(S["a1_pv"], g + 1)
                act.activation(a1_sq[:, :], ps_o[:, 0:DV1], ACT.Square, scale=a1_rsum[:, par, 0:1],
                               accum_out=a1_ss[:, par:par + 1]).then_inc(S["a1_squared"], 1)

            def body(h, first, last):
                for s in range(SLOTS):
                    g = h * SLOTS + s
                    if not (first and s < 3):
                        ot_out(g - 3, (s - 3) % 2)
                    softmax(g, s % 2, 0)
                    if not (first and s < 2):
                        sum_square(g - 2, s % 2)
                    pieces = a1_pieces(s, last)
                    if pieces:
                        a1_act_piece(act, a1_splits(h, s, last, 1), pieces[0])
                    if not (first and s < 2):
                        norm_o(g - 2, s % 2)
                    if not (first and s < 1):
                        at_hi(g - 1)
                    if len(pieces) > 1:
                        a1_act_piece(act, a1_splits(h, s, last, 2), pieces[1])
                    softmax(g, s % 2, 1)

            heads(act, H1, body)
            g = H1 * SLOTS
            ot_out(g - 3, 1)
            sum_square(g - 2, 0)
            at_hi(g - 1)
            norm_o(g - 2, 0)
            ot_out(g - 2, 0)
            sum_square(g - 1, 1)
            norm_o(g - 1, 1)
            ot_out(g - 1, 1)

        def a1_dve(dve):
            for i, (kind, half) in enumerate(A1_FIRST):
                a1_dve_piece(dve, i + 1, (kind, 0, half), first_bank(i))
                if i == A1_TURN_AFTER:
                    turn_dve(dve, TURN_F0 + NC - 1, NC - 1, ps_t[:, (NC - 1) % 2, :])
            dve.wait_ge(S["y_zero"], 2)

            def negmax(g, par, m):
                dve.wait_ge(S["a1_scores"], 2 * g + (m + 1))
                dve.tensor_reduce(a1_negmax[:, par, m:m + 1], ps_s[:, m, :, :], AX.XY, ALU.max, negate=True)\
                    .then_inc(S["a1_negmaxed"], 1)

            def at_lo(g):
                for half in range(2):
                    dve.wait_ge(S["a1_pt_hi"], 2 * g + (half + 1))
                    tiles = slice(half * 4, half * 4 + 4)
                    dve.tensor_tensor(a1_atl[:, tiles, :], ps_t[:, half, :].rearrange("p (t c) -> p t c", c=P),
                                      a1_ath[:, tiles, :], ALU.subtract).then_inc(S["a1_pt_lo"], 1)

            def add_out(g, tok_tile):
                dve.wait_ge(S["a1_out_in"], g + 1)
                y = Y[:, tok_tile, :]
                dve.tensor_tensor(y, ps_m[:, 2 * P:3 * P], y, ALU.add).then_inc(S["a1_added"], 1)

            def factors(g, h, par):
                dve.wait_ge(S["a1_exped"], 2 * g + 2)
                dve.wait_ge(S["a1_combined"], from0(g - 1))
                dve.wait_ge(S["a1_o_normed"], from0(g - 1))
                dve.reciprocal(a1_rsum[:, par, :], a1_sum[:, par, :]).then_inc(S["a1_rsummed"], 1)
                dve.wait_ge(S["a1_rsummed"], g + 1)
                dve.sem_inc(S["waited"], 1)
                dve.scalar_tensor_tensor(out=a1_c[:, par:par + 1], in0=a1_rsum[:, par, 1:2],
                                         scalar=a1_sum[:, par, 0:1], in1=a1_neglam[:, bass.ds(h, 1)],
                                         op0=ALU.mult, op1=ALU.mult).then_inc(S["a1_c_ready"], 1)

            def combine(g, par):
                dve.wait_ge(S["a1_c_ready"], g + 1)
                p1, p2 = (a1_p[par][m][:, :] for m in range(2))
                dve.scalar_tensor_tensor(out=p1, in0=p2, scalar=a1_c[:, par:par + 1], in1=p1,
                                         op0=ALU.mult, op1=ALU.add).then_inc(S["a1_combined"], 1)

            def body(h, first, last):
                for s in range(SLOTS):
                    g = h * SLOTS + s
                    negmax(g, s % 2, 0)
                    if not (first and s < 1):
                        factors(g - 1, h if s else h - 1, (s - 1) % 2)
                    if not (first and s < 3):
                        add_out(g - 3, (s - 3) % SLOTS)
                    if not (first and s < 1):
                        combine(g - 1, (s - 1) % 2)
                    pieces = a1_pieces(s, last)
                    if pieces:
                        a1_dve_piece(dve, a1_splits(h, s, last, 1), pieces[0])
                    negmax(g, s % 2, 1)
                    if not (first and s < 1):
                        at_lo(g - 1)
                    if len(pieces) > 1:
                        a1_dve_piece(dve, a1_splits(h, s, last, 2), pieces[1])
                    if last and s >= KT + 3:
                        if s == KT + 3:
                            dve.wait_ge(S["a1_added"], h * SLOTS + KT)
                        norm_pair(dve, s - (KT + 3), NORM_A1, 0, lambda i, k: tile(Y, i * TPC + k))

            heads(dve, H1, body)
            g = H1 * SLOTS
            factors(g - 1, H1 - 1, 1)
            combine(g - 1, 1)
            add_out(g - 3, SLOTS - 3)
            at_lo(g - 1)
            add_out(g - 2, SLOTS - 2)
            add_out(g - 1, SLOTS - 1)

        def a1_weights(pool, count, h, b):
            pool.wait_ge(S["a1_w_loaded"][b], h * 16 + 16)
            pool.sem_inc(S["waited"], 1)
            pool.tensor_scalar(a1_w_hi[b][:, :], a1_w_raw[b][:, :], 1.0, 0.0, ALU.mult, ALU.add)\
                .then_inc(S["a1_w_hi"], 1)
            pool.wait_ge(S["a1_w_hi"], count)
            pool.tensor_tensor(a1_w_lo[b][:, :], a1_w_raw[b][:, :], a1_w_hi[b][:, :], ALU.subtract)\
                .then_inc(S["a1_w_lo"], 1)

        def a1_pool(pool):
            def out_weights(h, b):
                if b == 0:
                    pool.wait_ge(S["a1_wo_loaded"], h * 16 + 16)
                    pool.sem_inc(S["waited"], 1)
                for j in range(2):
                    ins = pool.tensor_scalar(a1_wo[b][:, j, :], a1_wo_raw[:, j, :], a1_rms[:, j:j + 1],
                                             1.0 - LAMBDA_INIT, ALU.mult, ALU.mult)
                ins.then_inc(S["a1_wo_scaled"], 1)

            pool.wait_ge(S["x_turned"], TURN_F0 + NC)
            pool.memset(Y[:, :, :], 0.0).then_inc(S["y_zero"], 1)
            pool.wait_ge(S["a1_rms_loaded"], 16)
            out_weights(0, 0)

            def rms(g, par):
                pool.wait_ge(S["a1_squared"], g + 1)
                pool.sem_inc(S["waited"], 1)
                r = a1_r[:, par:par + 1]
                pool.tensor_scalar(r, a1_ss[:, par:par + 1], 1.0 / DV1, EPS_RMS1, ALU.mult, ALU.add).then_inc(S["a1_rms_eps"], 1)
                pool.wait_ge(S["a1_rms_eps"], g + 1)
                pool.tensor_tensor(r, r, minus_half[:, 0:1], ALU.pow).then_inc(S["a1_rms_power"], 1)
                pool.wait_ge(S["a1_rms_power"], g + 1)
                pool.tensor_tensor(r, r, a1_rsum[:, par, 0:1], ALU.mult).then_inc(S["a1_rms_ready"], 1)

            def body(h, first, last):
                for s in range(SLOTS):
                    g = h * SLOTS + s
                    if not (first and s < 2):
                        rms(g - 2, s % 2)
                    if s == 1 and not last:
                        pool.wait_ge(S["a1_split_in"], a1_splits(h, -1, last))
                        a1_weights(pool, 2 * h + 3, h + 1, 0)
                    if s == 3:
                        pool.wait_ge(S["a1_out_in"], h * SLOTS)
                        pool.sem_inc(S["waited"], 1)
                        out_weights(h, 1)
                    if s == KT + 1 and not last:
                        pool.wait_ge(S["a1_split_in"], a1_splits(h, KT - 1, last))
                        a1_weights(pool, 2 * h + 4, h + 1, 1)
                    if s == KT + 3 and not last:
                        pool.wait_ge(S["a1_out_in"], h * SLOTS + KT)
                        pool.sem_inc(S["waited"], 1)
                        out_weights(h + 1, 0)
                    if last and s in (KT + 3, KT + 6):
                        for i in range(2):
                            norm_rstd(pool, NORM_A1 + (0 if s == KT + 3 else 2) + i, i)
                    if last and s >= KT + 3:
                        f1_weights(pool, s - (KT + 3))

            heads(pool, H1, body)
            rms(H1 * SLOTS - 2, 0)
            rms(H1 * SLOTS - 1, 1)
            f1_weights(pool, 5)

        def a1_sp(sp):
            sp.wait_ge(S["f0_w1_lo_ready"], NE)
            for b in range(B):
                sp.dma_start(a1_w_raw[b][:, :], t["l1_w"][0]).then_inc(S["a1_w_loaded"][b], 16)
            sp.dma_start(a1_lam[:, :, :], t["l1_lam"]).then_inc(S["a1_lam_loaded"], 16)
            sp.dma_start(a1_rms[:, :], t["l1_rms"]).then_inc(S["a1_rms_loaded"], 16)
            wo_raw = a1_wo_raw[:, :, :].rearrange("p a b -> p (a b)")
            sp.dma_start(wo_raw, t["l1_wo"][0]).then_inc(S["a1_wo_loaded"], 16)

            def body(h, first, last):
                if last:
                    return
                for b in range(B):
                    sp.wait_ge(S["a1_w_lo"], 2 * h + (b + 1))
                    sp.dma_start(a1_w_raw[b][:, :], row(t["l1_w"], h + 1)).then_inc(S["a1_w_loaded"][b], 16)
                sp.wait_ge(S["a1_wo_scaled"], 2 * h + 2)
                sp.dma_start(wo_raw, row(t["l1_wo"], h + 1)).then_inc(S["a1_wo_loaded"], 16)

            heads(sp, H1, body)

        F1_PRE = 4 * HT
        F1_HIDDEN = 4 * HT
        F1_SPLIT = 6 * HT

        def f1_weights(pool, part):
            n = f1_w.shape[1] // 6 + 1
            ws = slice(part * n, min((part + 1) * n, f1_w.shape[1]))
            if part == 0:
                pool.wait_ge(S["f1_loaded"], 32)
            pool.tensor_scalar(f1_w[:, ws], f1_raw[:, ws], 1.0, 0.0, ALU.mult, ALU.add).then_inc(S["f1_w_ready"], 1)

        def f1_bank(use):
            return ps_s[:, use % 4 // 2, use % 2, :]

        def f1_pairs(body):
            body(0, True)
            body(1, False)

        def f1_pe(pe):
            for c in range(2):
                pe.wait_ge(S["xst_ready"], 2 * NC + c + 1)
                turn_pe(pe, TURN_A1 + c, c, lambda i: xst[c % 2][:, i, :])
            pe.wait_ge(S["f1_w_ready"], 6)

            def first_layer(p, i):
                pe.wait_ge(S["x_lo"], TURN_A1 + 2 * p + i + 1)
                x = slice((2 * p + i) * BANK, (2 * p + i + 1) * BANK)
                for ht in range(HT):
                    for w in range(2):
                        use = 2 * HT * i + 2 * ht + w
                        if use >= 4:
                            pe.wait_ge((S["f1_silued"], S["f1_gated"])[w], p * 2 * HT + (use - 4) // 2 + 1)
                        elif p:
                            pe.wait_ge(S["f1_gelued"], p * F1_HIDDEN)
                        cols = slice(ht * P, (ht + 1) * P)
                        pe.matmul(f1_bank(use), f1_w12[:, w, cols], xT_hi[:, x], start=True, stop=False)
                        pe.matmul(f1_bank(use), f1_w12[:, w, cols], xT_lo[:, x], start=False, stop=True)\
                            .then_inc(S["f1_pre"], 1)

            def hidden_layer(p, layer, i):
                for ot in range(HT):
                    k = 2 * HT * layer + HT * i + ot
                    if k < 4:
                        pe.wait_ge((S["f1_silued"], S["f1_gated"])[k % 2], p * 2 * HT + (F1_PRE - 4 + k) // 2 + 1)
                    else:
                        pe.wait_ge(S["f1_gelued"], p * F1_HIDDEN + (k - 3))
                    cols = slice(ot * P, (ot + 1) * P)
                    for kt in range(HT):
                        if ot == 0:
                            pe.wait_ge(S["f1_split"], p * F1_SPLIT + 2 * HT * layer + HT * i + kt + 1)
                        w = f1_wh[:, layer, kt, cols]
                        pe.matmul(f1_bank(k), w, f1_hi[i][layer][kt][:, :], start=kt == 0, stop=False)
                        ins = pe.matmul(f1_bank(k), w, f1_lo[i][layer][kt][:, :], start=False, stop=kt == HT - 1)
                    ins.then_inc(S["f1_hidden"], 1)

            def last_layer(p, i):
                pe.wait_ge(S["f1_y_out"], 2 * p)
                bank = (ps_o, ps_m)[i]
                for kt in range(HT):
                    pe.wait_ge(S["f1_split"], p * F1_SPLIT + 4 * HT + HT * i + kt + 1)
                    pe.matmul(bank[:, :], f1_w3[:, kt, :], f1_hi[i][0][kt][:, :], start=kt == 0, stop=False)
                    ins = pe.matmul(bank[:, :], f1_w3[:, kt, :], f1_lo[i][0][kt][:, :], start=False, stop=kt == HT - 1)
                ins.then_inc(S["f1_down"], 1)

            def turn_back(p, i):
                pe.wait_ge(S["f1_y_out"], 2 * p + i + 1)
                pe.wait_ge(S["f1_y_used"], 2 * p)
                for k in range(TPC):
                    ins = pe.transpose(ps_t[:, i, k * P:(k + 1) * P], f1_y[i][:, k * P:(k + 1) * P], ident[:, :])
                ins.then_inc(S["f1_y_turned"], 1)

            def body(p, first):
                for i in range(2):
                    first_layer(p, i)
                for i in range(2):
                    hidden_layer(p, 0, i)
                if first:
                    for c in range(2, NC):
                        pe.wait_ge(S["xst_ready"], 2 * NC + c + 1)
                        turn_pe(pe, TURN_A1 + c, c, lambda i: xst[c % 2][:, i, :])
                for i in range(2):
                    hidden_layer(p, 1, i)
                for i in range(2):
                    last_layer(p, i)
                for i in range(2):
                    turn_back(p, i)

            f1_pairs(body)

        def f1_act(act):
            for c in range(2):
                turn_act(act, TURN_A1 + c, c)
            act.wait_ge(S["f1_s_loaded"], 16)

            def silu(p, j):
                act.wait_ge(S["f1_pre"], p * F1_PRE + 2 * j + 1)
                act.wait_ge(S["f1_gated"], max(p * 2 * HT + (j - 1), 0))
                ht = j % HT
                act.activation(f1_a[j % 2][:, :], f1_bank(2 * j), ACT.Silu, scale=f1_s[:, ht:ht + 1])\
                    .then_inc(S["f1_silued"], 1)

            def gelu(p, layer, i, ot):
                k = 2 * HT * layer + HT * i + ot
                item = 2 * HT + k
                scale = f1_s[:, HT * (layer + 2) + ot:HT * (layer + 2) + ot + 1]
                act.wait_ge(S["f1_hidden"], p * F1_HIDDEN + k + 1)
                act.wait_ge(S["f1_split"], p * F1_SPLIT + item - 3)
                act.activation(f1_f[item % 4][:, :], f1_bank(k), ACT.Gelu, scale=scale)
                act.activation(f1_hi[i][1 - layer][ot][:, :], f1_bank(k), ACT.Gelu, scale=scale)\
                    .then_inc(S["f1_gelued"], 1)

            def body(p, first):
                for j in range(2 * HT):
                    silu(p, j)
                for i in range(2):
                    for ot in range(HT):
                        gelu(p, 0, i, ot)
                if first:
                    for c in range(2, NC):
                        turn_act(act, TURN_A1 + c, c)
                for i in range(2):
                    for ot in range(HT):
                        gelu(p, 1, i, ot)
                for i in range(2):
                    act.wait_ge(S["f1_down"], 2 * p + i + 1)
                    act.wait_ge(S["f1_y_turned"], 2 * p)
                    act.activation(f1_y[i][:, :], (ps_o, ps_m)[i][:, :], ACT.Copy, scale=f1_s[:, 4 * HT:4 * HT + 1])\
                        .then_inc(S["f1_y_out"], 1)

            f1_pairs(body)

        def f1_dve(dve):
            for c in range(2):
                turn_dve(dve, TURN_A1 + c, c, ps_t[:, c % 2, :])

            def gate(p, j):
                dve.wait_ge(S["f1_silued"], p * 2 * HT + j + 1)
                dve.wait_ge(S["f1_pre"], p * F1_PRE + 2 * j + 2)
                dve.wait_ge(S["f1_split"], max(p * F1_SPLIT + (j - 3), 0))
                ht = j % HT
                dve.scalar_tensor_tensor(out=f1_f[j % 4][:, :], in0=f1_bank(2 * j + 1), scalar=f1_s[:, HT + ht:HT + ht + 1],
                                         in1=f1_a[j % 2][:, :], op0=ALU.mult, op1=ALU.mult).then_inc(S["f1_gated"], 1)

            def low(p, item):
                stage, i, kt = item // (2 * HT), item // HT % 2, item % HT
                if stage == 0:
                    dve.wait_ge(S["f1_hi_ready"], p * 2 * HT + item + 1)
                else:
                    dve.wait_ge(S["f1_gelued"], p * F1_HIDDEN + (item - 2 * HT) + 1)
                dve.tensor_tensor(f1_lo[i][stage % 2][kt][:, :], f1_f[item % 4][:, :], f1_hi[i][stage % 2][kt][:, :],
                                  ALU.subtract).then_inc(S["f1_split"], 1)

            def body(p, first):
                for j in range(2 * HT):
                    gate(p, j)
                    if j:
                        low(p, j - 1)
                low(p, 2 * HT - 1)
                if first:
                    dve.wait_ge(S["a1_added"], H1 * SLOTS)
                    for stage in range(5):
                        norm_pair(dve, stage, NORM_A1 + 4, 2, lambda i, k: tile(Y, (2 + i) * TPC + k))
                for item in range(2 * HT, 4 * HT):
                    low(p, item)
                if first:
                    for c in range(2, NC):
                        turn_dve(dve, TURN_A1 + c, c, ps_t[:, c % 2, :])
                for item in range(4 * HT, 6 * HT):
                    low(p, item)
                n = NORM_F1 + 2 * p
                for i in range(2):
                    dve.wait_ge(S["f1_y_turned"], 2 * p + i + 1)
                    norm_stats(dve, n + i, i, lambda k: bank_tile(ps_t[:, i, :], k))
                dve.wait_ge(S["x_final"], 2 * p)
                for i in range(2):
                    norm_apply(dve, n + i, i, lambda k: bank_tile(ps_t[:, i, :], k), lambda k: tile(xst[i], k))\
                        .then_inc(S["f1_y_used"], 1)
                for i in range(2):
                    dve.wait_ge(S["f1_y_used"], 2 * p + i + 1)
                    xc = X[:, (2 * p + i) * TPC:(2 * p + i + 1) * TPC, :]
                    dve.tensor_tensor(xc, xc, xst[i][:, :, :], ALU.add).then_inc(S["x_final"], 1)

            f1_pairs(body)

        def f1_pool(pool):
            def body(p, first):
                for j in range(2 * HT):
                    pool.wait_ge(S["f1_gated"], p * 2 * HT + j + 1)
                    pool.tensor_scalar(f1_hi[j // HT][0][j % HT][:, :], f1_f[j % 4][:, :], 1.0, 0.0, ALU.mult, ALU.add)\
                        .then_inc(S["f1_hi_ready"], 1)
                if first:
                    for k in range(4):
                        norm_rstd(pool, NORM_A1 + 4 + k, 2 + k % 2)
                for i in range(2):
                    norm_rstd(pool, NORM_F1 + 2 * p + i, i)

            f1_pairs(body)

        def f1_load_sp(sp):
            sp.wait_ge(S["a1_scores"], 2 * (H1 - 1) * SLOTS + 2 * KT)
            half = f1_raw.shape[1] // 2
            sp.dma_start(f1_raw[:, 0:half], t["ffn1_w"][:, 0:half]).then_inc(S["f1_loaded"], 16)
            sp.dma_start(f1_raw[:, half:], t["ffn1_w"][:, half:]).then_inc(S["f1_loaded"], 16)
            sp.dma_start(f1_s[:, :], t["ffn1_s"]).then_inc(S["f1_s_loaded"], 16)

        def f1_sp(sp):
            for c in range(NC):
                sp.wait_ge(S["x_final"], c + 1)
                sp.dma_start(out_dram[:, c * TPC:(c + 1) * TPC, :], X[:, c * TPC:(c + 1) * TPC, :])\
                    .then_inc(S["out_stored"], 16)
            sp.wait_ge(S["out_stored"], 16 * NC)

        block = ctx.enter_context(nc.Block())

        @block.vector
        def _(dve):
            input_dve(dve)
            a0_dve(dve)
            f0_pre_dve(dve)
            f0_dve(dve)
            a1_dve(dve)
            f1_dve(dve)

        @block.tensor
        def _(pe):
            input_pe(pe)
            a0_pe(pe)
            f0_pre_pe(pe)
            f0_pe(pe)
            a1_pe(pe)
            f1_pe(pe)

        @block.scalar
        def _(act):
            input_act(act)
            a0_act(act)
            f0_pre_act(act)
            f0_act(act)
            a1_act(act)
            f1_act(act)

        @block.gpsimd
        def _(pool):
            input_pool(pool)
            a0_pool(pool)
            f0_pre_pool(pool)
            f0_pool(pool)
            a1_pool(pool)
            f1_pool(pool)

        @block.sync
        def _(sp):
            input_sp(sp)
            a0_sp(sp)
            f0_sp(sp)
            a1_sp(sp)
            f1_load_sp(sp)
            f1_sp(sp)


def kernel(**inputs):
    import numpy as np
    import concourse.bacc as bacc
    from concourse import mybir as mb
    from concourse.bass_utils import run_bass_kernel_spmd

    w = {k: np.asarray(v) for k, v in inputs.items()}
    D, H0, DH0, H1, HID, E = 128, 16, 64, 8, 512, 8
    qkv = w["L0_attn_W_qkv"].reshape(D, H0, DH0, 3).transpose(3, 1, 0, 2)
    wo0 = w["L0_attn_W_out"].reshape(H0, DH0, D)
    w1 = np.concatenate([w["L0_ffn_ew1"], w["L0_ffn_sw1"][None]])
    w2 = np.concatenate([w["L0_ffn_ew2"], w["L0_ffn_sw2"][None]])
    b1 = np.concatenate([w["L0_ffn_eb1"], w["L0_ffn_sb1"][None]])
    b2 = np.concatenate([w["L0_ffn_eb2"], w["L0_ffn_sb2"][None]])
    by_head = lambda a: a.reshape(H1, 2 * D, D).transpose(0, 2, 1)
    q, k, v = (by_head(w[f"L1_attn_W{n}"]) for n in "qkv")
    lam = np.stack([w[f"L1_attn_lambda_{n}"].T for n in ("q1", "k1", "q2", "k2")], axis=1)
    tiled = lambda a: a.T.reshape(-1, D, a.shape[0]).transpose(1, 0, 2).reshape(D, -1)
    col = lambda a: a.reshape(-1, D).T
    arrays = {
        "x": w["L0_attn_X"],
        "l0_wqk": np.concatenate([qkv[0], qkv[1]], axis=2),
        "l0_wv": np.concatenate([qkv[2], qkv[2]], axis=2),
        "l0_wo": np.concatenate([wo0, wo0], axis=1),
        "ffn0_w1": w1.transpose(1, 0, 2),
        "ffn0_w2": w2.reshape(E + 1, HID // D, D, D).transpose(2, 0, 1, 3),
        "ffn0_b1": b1.reshape(E + 1, HID // D, D).transpose(2, 0, 1),
        "ffn0_b2": b2,
        "ffn0_nw": w["L0_ffn_norm_weight"].reshape(D, 1),
        "ffn0_rw": w["L0_ffn_router_w"].T,
        "l1_w": np.concatenate([q, k, v], axis=2),
        "l1_wo": w["L1_attn_Wo"].reshape(D, H1, 2, D).transpose(1, 3, 2, 0).reshape(H1, D, 2 * D),
        "l1_lam": lam,
        "l1_rms": col(w["L1_attn_rms_scale"]),
        "ffn1_w": np.concatenate([tiled(w[f"L1_ffn_{n}_w"]) for n in ("w1", "w2", "h1", "h2", "w3")], axis=1),
        "ffn1_s": np.concatenate([col(w[f"L1_ffn_{n}_s"]) for n in ("w1", "w2", "h1", "h2", "w3")], axis=1),
    }
    arrays = {k: np.ascontiguousarray(a) for k, a in arrays.items()}
    nc = bacc.Bacc("TRN2", target_bir_lowering=False, num_devices=1)
    aps = {k: nc.dram_tensor(f"in_{k}", a.shape, mb.dt.from_np(a.dtype), kind="ExternalInput").ap()
           for k, a in arrays.items()}
    out = nc.dram_tensor("out", w["L0_attn_X"].shape, mb.dt.from_np(np.dtype("float32")), kind="ExternalOutput").ap()
    sandwich_kernel(nc, aps, out)
    r = run_bass_kernel_spmd(nc, [{f"in_{k}": a for k, a in arrays.items()}], core_ids=[0])
    return r.results[0]["out"]
```
